# Optimizing a Trainium2 kernel written in Bass

```python
import numpy as np
import jax
import jax.numpy as jnp

def _softmax(x, axis=-1):
    return jax.nn.softmax(x, axis=axis)

def _gelu(x):
    return jax.nn.gelu(x, approximate=True)

def _silu(x):
    return jax.nn.silu(x)

def _sigmoid(x):
    return jax.nn.sigmoid(x)

def _layernorm(x, axis=-1, eps=1e-05):
    m = jnp.mean(x, axis=axis, keepdims=True)
    v = jnp.var(x, axis=axis, keepdims=True)
    return (x - m) / jnp.sqrt(v + eps)

def _scatter_add(tgt, idx, src, axis=0):
    return tgt.at[idx].add(src)

def _segment_sum(src, seg, n):
    return jax.ops.segment_sum(src, seg, n)
kernel_name = 'mk_adj_seq_d2_adj_r2_e6bbbb'

def setup_inputs(seed: int=0):
    np.random.seed(seed)
    _w = jnp.asarray

    def _rec_inputs():
        import jax
        import jax.numpy as jnp
        _gk = jax.random.key(seed)
        x = -0.0005207 + 1.001 * jax.random.normal(jax.random.fold_in(_gk, 1), (128, 64, 128), jnp.float32)
        _a = jax.random.bernoulli(jax.random.fold_in(_gk, 2), 0.0625, (128, 64, 64))
        _a = jnp.logical_or(_a, jnp.swapaxes(_a, -1, -2))
        _a = jnp.logical_or(_a, jnp.eye(64, dtype=bool))
        _af = _a.astype(jnp.float32)
        _af = _af * jax.random.uniform(jax.random.fold_in(_gk, 3), (128, 64, 64), jnp.float32, 0.05, 0.000488281)
        adj = _af
        return (x, adj)
    x, adj = _rec_inputs()

    def _L0_gnn_setup():
        import jax, jax.numpy as jnp
        import numpy as np
        EPS = 0.001
        key = jax.random.key(seed)
        k1, k2, k3, k4 = jax.random.split(key, 4)
        B, N, F = (8, 1024, 128)
        x = jax.random.normal(k1, (B, N, F), dtype=jnp.float32)
        a = jax.random.uniform(k2, (B, N, N), dtype=jnp.float32) / N
        W = jax.random.normal(k3, (F, F), dtype=jnp.float32) * (1.0 / np.sqrt(F))
        b = jnp.zeros((F,), dtype=jnp.float32)
        gamma = jnp.ones((F,), dtype=jnp.float32)
        beta = jnp.zeros((F,), dtype=jnp.float32)
        return {'x': x, 'a': a, 'W': W, 'b': b, 'gamma': gamma, 'beta': beta}
    _L0_gnn_all = _L0_gnn_setup()
    _L0_gnn_in = {k: v for k, v in _L0_gnn_all.items() if k in ('W', 'b', 'gamma', 'beta')}
    del _L0_gnn_all

    def _L1_gnn_setup():
        import jax, jax.numpy as jnp
        import numpy as np
        B, N, D, H = (32, 64, 128, 128)
        LN_EPS = 1e-05

        def _mlp(x, W1, b1, g, beta, W2, b2):
            h = x @ W1 + b1
            mu = jnp.mean(h, axis=-1, keepdims=True)
            var = jnp.var(h, axis=-1, keepdims=True)
            h = (h - mu) * jax.lax.rsqrt(var + LN_EPS) * g + beta
            h = jax.nn.gelu(h, approximate=False)
            return h @ W2 + b2
        key = jax.random.key(seed)
        ks = jax.random.split(key, 10)
        s = lambda fan_in: 1.0 / np.sqrt(fan_in)
        return {'slots': jax.random.normal(ks[0], (B, N, D), dtype=jnp.float32), 'adjacency': jax.random.uniform(ks[1], (B, N, N), dtype=jnp.float32), 'We1': jax.random.uniform(ks[2], (2 * D, H), minval=-s(2 * D), maxval=s(2 * D), dtype=jnp.float32), 'be1': jnp.zeros((H,), jnp.float32), 'ge': jnp.ones((H,), jnp.float32), 'bge': jnp.zeros((H,), jnp.float32), 'We2': jax.random.uniform(ks[3], (H, D), minval=-s(H), maxval=s(H), dtype=jnp.float32), 'be2': jnp.zeros((D,), jnp.float32), 'Wn1': jax.random.uniform(ks[4], (2 * D, H), minval=-s(2 * D), maxval=s(2 * D), dtype=jnp.float32), 'bn1': jnp.zeros((H,), jnp.float32), 'gn': jnp.ones((H,), jnp.float32), 'bgn': jnp.zeros((H,), jnp.float32), 'Wn2': jax.random.uniform(ks[5], (H, D), minval=-s(H), maxval=s(H), dtype=jnp.float32), 'bn2': jnp.zeros((D,), jnp.float32)}
    _L1_gnn_all = _L1_gnn_setup()
    _L1_gnn_in = {k: v for k, v in _L1_gnn_all.items() if k in ('We1', 'be1', 'ge', 'bge', 'We2', 'be2', 'Wn1', 'bn1', 'gn', 'bgn', 'Wn2', 'bn2')}
    del _L1_gnn_all
    return {'x': x, 'adj': adj, 'L0_gnn_W': _L0_gnn_in['W'], 'L0_gnn_b': _L0_gnn_in['b'], 'L0_gnn_gamma': _L0_gnn_in['gamma'], 'L0_gnn_beta': _L0_gnn_in['beta'], 'L1_gnn_We1': _L1_gnn_in['We1'], 'L1_gnn_be1': _L1_gnn_in['be1'], 'L1_gnn_ge': _L1_gnn_in['ge'], 'L1_gnn_bge': _L1_gnn_in['bge'], 'L1_gnn_We2': _L1_gnn_in['We2'], 'L1_gnn_be2': _L1_gnn_in['be2'], 'L1_gnn_Wn1': _L1_gnn_in['Wn1'], 'L1_gnn_bn1': _L1_gnn_in['bn1'], 'L1_gnn_gn': _L1_gnn_in['gn'], 'L1_gnn_bgn': _L1_gnn_in['bgn'], 'L1_gnn_Wn2': _L1_gnn_in['Wn2'], 'L1_gnn_bn2': _L1_gnn_in['bn2']}

def reference(x, adj, L0_gnn_W, L0_gnn_b, L0_gnn_gamma, L0_gnn_beta, L1_gnn_We1, L1_gnn_be1, L1_gnn_ge, L1_gnn_bge, L1_gnn_We2, L1_gnn_be2, L1_gnn_Wn1, L1_gnn_bn1, L1_gnn_gn, L1_gnn_bgn, L1_gnn_Wn2, L1_gnn_bn2):
    import jax
    import jax.numpy as jnp

    def _L0_gnn_ref(x, a, W, b, gamma, beta):
        import jax, jax.numpy as jnp
        import numpy as np
        EPS = 0.001
        h = jnp.einsum('bnm,bmf->bnf', a, x @ W) + b
        mu = jnp.mean(h, axis=1, keepdims=True)
        var = jnp.var(h, axis=1, keepdims=True)
        hn = (h - mu) * jax.lax.rsqrt(var + EPS) * gamma + beta
        s = hn * jax.nn.sigmoid(hn)
        return s + x

    def _L1_gnn_ref(slots, adjacency, We1, be1, ge, bge, We2, be2, Wn1, bn1, gn, bgn, Wn2, bn2):
        import jax, jax.numpy as jnp
        import numpy as np
        B, N, D, H = (32, 64, 128, 128)
        LN_EPS = 1e-05

        def _mlp(x, W1, b1, g, beta, W2, b2):
            h = x @ W1 + b1
            mu = jnp.mean(h, axis=-1, keepdims=True)
            var = jnp.var(h, axis=-1, keepdims=True)
            h = (h - mu) * jax.lax.rsqrt(var + LN_EPS) * g + beta
            h = jax.nn.gelu(h, approximate=False)
            return h @ W2 + b2
        b, n, d = slots.shape
        ei = jnp.broadcast_to(slots[:, :, None, :], (b, n, n, d))
        ej = jnp.broadcast_to(slots[:, None, :, :], (b, n, n, d))
        edge_feat = jnp.concatenate([ei, ej], axis=-1)
        edge_out = _mlp(edge_feat, We1, be1, ge, bge, We2, be2)
        mask = 1.0 - jnp.eye(n, dtype=slots.dtype)
        w = adjacency * mask
        messages = jnp.einsum('bij,bijd->bid', w, edge_out)
        node_input = jnp.concatenate([slots, messages], axis=-1)
        delta = _mlp(node_input, Wn1, bn1, gn, bgn, Wn2, bn2)
        return slots + delta
    x = _L0_gnn_ref(x, adj, L0_gnn_W, L0_gnn_b, L0_gnn_gamma, L0_gnn_beta)
    x = _L1_gnn_ref(x, adj, L1_gnn_We1, L1_gnn_be1, L1_gnn_ge, L1_gnn_bge, L1_gnn_We2, L1_gnn_be2, L1_gnn_Wn1, L1_gnn_bn1, L1_gnn_gn, L1_gnn_bgn, L1_gnn_Wn2, L1_gnn_bn2)
    return x

_drawn_inputs = setup_inputs


def setup_inputs(seed=0):
    import zlib

    import numpy as np

    out = dict(_drawn_inputs(seed))
    spreads = {'L0_gnn_b': (0.0, 0.8),
     'L0_gnn_gamma': (1.0, 0.2),
     'L0_gnn_beta': (0.0, 0.1),
     'L1_gnn_be1': (0.0, 0.8),
     'L1_gnn_ge': (1.0, 0.6),
     'L1_gnn_bge': (0.0, 0.8),
     'L1_gnn_be2': (0.0, 0.713),
     'L1_gnn_bn1': (0.0, 0.1),
     'L1_gnn_gn': (1.0, 0.2),
     'L1_gnn_bgn': (0.0, 0.27),
     'L1_gnn_bn2': (0.0, 0.1)}
    factors = {}
    for name, (base, spread) in spreads.items():
        noise = np.random.default_rng([zlib.crc32(name.encode()), seed]).standard_normal(out[name].shape)
        drawn = base * np.exp(spread * noise) if base else spread * noise
        out[name] = jnp.asarray(drawn.astype(out[name].dtype))
    for name, factor in factors.items():
        out[name] = (out[name] * factor).astype(out[name].dtype)
    return out
```

```python
from contextlib import ExitStack

import numpy as np

import concourse.bass as bass
from concourse import mybir

F32 = mybir.dt.float32
F32R = mybir.dt.float32r
ACT = mybir.ActivationFunctionType
ALU = mybir.AluOpType
AX = mybir.AxisListType

P = 128
NB = 128
N = 64
D = 128
GB = 4
NG = NB // GB
JH = 2
JW = N // JH
Q = P // JW
T = N // Q
GE = JH * GB * T
CH = 512
NC = NB * N // CH
PAIRS = CH // P
EPS0, EPS1 = 1e-3, 1e-5

C_ID, C_OFF, C_OFFE, C_CEN, C_BM, C_SEL = 0, 128, 256, 384, 512, 520
C_ALL = C_SEL + JH * T * P


def constants():
    c = np.zeros((P, C_ALL), np.float32)
    eye = np.eye(P, dtype=np.float32)
    c[:, C_ID:C_ID + P] = eye
    c[:, C_OFF:C_OFF + P] = 1 - eye
    c[:, C_CEN:C_CEN + P] = eye - 1.0 / D
    e = np.arange(P)
    q, jj = e // JW, e % JW
    for jh in range(JH):
        for g in range(GB):
            for t in range(T):
                c[:, C_OFFE + (jh * GB + g) * T + t] = Q * t + q != JW * jh + jj
    for base in (0, 32):
        for part in range(4):
            for g in range(GB):
                c[base + GB * part + g, C_BM + g] = part % 2 == 0
                c[base + GB * part + g, C_BM + 4 + g] = part % 2 == 1
    sel = c[:, C_SEL:].reshape(P, JH, T, P)
    for jh in range(JH):
        for t in range(T):
            sel[Q * t + q, jh, t, e] = 1
            sel[N + JW * jh + jj, jh, t, e] = 1
    return c


def steps(eng, n, body, head, tail):
    assert head % 2 == 0 and (n - head - tail) % 2 == 0
    for k in range(head):
        body(k, k % 2, k // 2)
    with eng.Fori(0, (n - head - tail) // 2) as i:
        body(i * 2 + head, 0, i + head // 2)
        body(i * 2 + head + 1, 1, i + head // 2)
    for k in range(n - tail, n):
        body(k, k % 2, k // 2)


def build(nc, x, adj, consts, w, out):
    with ExitStack() as ctx:
        def sb(name, shape, dt=F32):
            return ctx.enter_context(nc.sbuf_tensor(name, shape, dt))

        def sem(name):
            return ctx.enter_context(nc.semaphore(name))

        bank = [ctx.enter_context(nc.psum_tensor(f"bank{i}", [P, 512], F32)) for i in range(8)]

        x1T = sb("x1T", [P, NB * N])
        hT = sb("hT", [P, NB * N])
        wE = sb("wE", [P, NG * GE])
        rE = sb("rE", [P, NG * GE])
        cst = sb("cst", [P, C_SEL])
        wt = {n: sb(n, [P, D]) for n in ("W", "Wa", "Wb", "We2", "Wna", "Wnb", "Wn2", "Wag", "Wbg")}
        ge_b = sb("ge_b", [P, D])
        bge_b = sb("bge_b", [P, D])
        be2_b = sb("be2_b", [P, D])
        cols = sb("cols", [P, 16])
        B0, GAM, BET, BE1, BN1, GN, BGN, BE1C, BN1C, EPSC, MEAN4 = 0, 1, 2, 3, 4, 5, 6, 7, 8, 9, 11
        bn2row = sb("bn2row", [1, D])
        be1row = sb("be1row", [1, D])
        ones = sb("ones", [P, D])
        ident = cst[:, C_ID:C_ID + P]
        sel = sb("sel", [P, JH * T * P], F32R)
        bgeR = sb("bgeR", [48, GB * D], F32R)
        big = sb("big", [P, 4 * 2048])
        wblk = sb("wblk", [P, JH * GB * T * 32])
        stdR = sb("stdR", [48, JH * T * P], F32R)
        Xf = sb("Xf", [P, GB * D])
        Xhi = [sb(f"Xhi{i}", [P, GB * D], F32R) for i in range(2)]
        Xlo = [sb(f"Xlo{i}", [P, GB * D], F32R) for i in range(2)]
        x1s = sb("x1s", [P, GB * N])
        gs = sb("gs", [P, 2 * D])
        stage = [sb(f"stage{i}", [P, CH]) for i in range(2)]

        adM_d = nc.dram_tensor("adM_d", [NC, P, CH], F32, kind="Internal").ap()
        s_d = nc.dram_tensor("s_d", [2, NG, GB, JH * T * P], F32, kind="Internal").ap()

        w_in, w_ready, w_psum, w_cols, w_row, w_done = map(sem, ("w_in", "w_ready", "w_psum", "w_cols", "w_row", "w_done"))
        col_of = {"L0_gnn_b": B0, "L0_gnn_gamma": GAM, "L0_gnn_beta": BET, "L1_gnn_be1": BE1,
                  "L1_gnn_bn1": BN1, "L1_gnn_gn": GN, "L1_gnn_bgn": BGN}
        with nc.Block() as block:
            @block.sync
            def _(sp):
                n = 0
                for dst, src in ([(cst[:], consts[:, 0:C_SEL]), (big[:, 0:4096], consts[:, C_SEL:C_ALL]),
                                  (wt["W"][:], w["L0_gnn_W"]), (wt["Wa"][:], w["L1_gnn_We1"][0:D, :]),
                                  (wt["Wb"][:], w["L1_gnn_We1"][D:2 * D, :]), (wt["We2"][:], w["L1_gnn_We2"]),
                                  (wt["Wna"][:], w["L1_gnn_Wn1"][0:D, :]), (wt["Wnb"][:], w["L1_gnn_Wn1"][D:2 * D, :]),
                                  (wt["Wn2"][:], w["L1_gnn_Wn2"]),
                                  (ge_b[:], w["L1_gnn_ge"].partition_broadcast(P)),
                                  (bge_b[:], w["L1_gnn_bge"].partition_broadcast(P)),
                                  (be2_b[:], w["L1_gnn_be2"].partition_broadcast(P)),
                                  (bn2row[:], w["L1_gnn_bn2"].unsqueeze(0))]
                                 + [(cols[:, c:c + 1], w[name].unsqueeze(1)) for name, c in col_of.items()]):
                    sp.dma_start(dst, src).then_inc(w_in, 16)
                    n += 16
                assert n == 16 * 20

            @block.tensor
            def _(pe):
                pe.wait_ge(w_in, 320)
                pe.matmul(bank[0][:, 0:2], cst[:, C_CEN:C_CEN + P], cols[:, BE1:BE1 + 2], start=True, stop=True).then_inc(w_psum, 1)
                pe.wait_ge(w_cols, 1)
                pe.matmul(bank[1][0:1, 0:D], cols[:, BE1C:BE1C + 1], ident, start=True, stop=True).then_inc(w_psum, 1)

            @block.scalar
            def _(act):
                act.wait_ge(w_in, 320)
                act.copy(sel[:], big[:, 0:4096]).then_inc(w_done, 1)

            @block.vector
            def _(v):
                v.memset(ones[:], 1.0)
                v.memset(wblk[:], 0.0)
                v.memset(cols[:, EPSC:EPSC + 1], EPS0)
                v.memset(cols[:, EPSC + 1:EPSC + 2], EPS1).then_inc(w_ready, 1)
                v.wait_ge(w_in, 320)
                r = 1
                for i, name in enumerate(("Wa", "Wb", "Wna", "Wnb")):
                    m = cols[:, MEAN4 + i:MEAN4 + i + 1]
                    v.tensor_reduce(m, wt[name][:], AX.X, ALU.add).then_inc(w_ready, 1)
                    v.wait_ge(w_ready, r + 1)
                    v.tensor_scalar(m, m, 1.0 / D, None, ALU.mult).then_inc(w_ready, 1)
                    v.wait_ge(w_ready, r + 2)
                    v.tensor_scalar(wt[name][:], wt[name][:], m, None, ALU.subtract).then_inc(w_ready, 1)
                    r += 3
                v.wait_ge(w_ready, r)
                v.tensor_tensor(wt["Wag"][:], wt["Wa"][:], ge_b[:], ALU.mult)
                v.tensor_tensor(wt["Wbg"][:], wt["Wb"][:], ge_b[:], ALU.mult)
                v.wait_ge(w_psum, 1)
                v.tensor_copy(cols[:, BE1C:BE1C + 2], bank[0][:, 0:2]).then_inc(w_cols, 1)
                v.wait_ge(w_psum, 2)
                v.tensor_tensor(be1row[:], bank[1][0:1, 0:D], ge_b[0:1, :], ALU.mult)
                hi, lo = bgeR[0:48, 0:D], big[0:48, 5200:5200 + D]
                v.tensor_copy(hi, bge_b[0:48, :]).then_inc(w_row, 1)
                v.wait_ge(w_row, 1)
                v.tensor_copy(big[0:48, 5000:5000 + D], hi.bitcast(F32)).then_inc(w_row, 1)
                v.wait_ge(w_row, 2)
                v.tensor_tensor(lo, bge_b[0:48, :], big[0:48, 5000:5000 + D], ALU.subtract).then_inc(w_row, 1)
                v.wait_ge(w_row, 3)
                for g in range(GB):
                    v.tensor_scalar(big[0:48, 6000 + 128 * g:6128 + 128 * g], big[0:48, 5000:5128],
                                    cst[0:48, C_BM + g:C_BM + g + 1], None, ALU.mult).then_inc(w_row, 1)
                v.wait_ge(w_row, 3 + GB)
                for g in range(GB):
                    v.scalar_tensor_tensor(out=bgeR[:, 128 * g:128 * g + 128], in0=lo,
                                           scalar=cst[0:48, C_BM + 4 + g:C_BM + 5 + g],
                                           in1=big[0:48, 6000 + 128 * g:6128 + 128 * g], op0=ALU.mult, op1=ALU.add)

        xin = [big[:, 0 + 512 * i:512 + 512 * i] for i in range(2)]
        adin = [big[:, 1024 + 512 * i:1536 + 512 * i] for i in range(2)]
        lin = [big[:, 2048 + 256 * i:2304 + 256 * i] for i in range(2)]
        adT = [big[:, 2560 + 512 * i:3072 + 512 * i] for i in range(2)]
        adM = [big[:, 3584 + 512 * i:4096 + 512 * i] for i in range(2)]
        yT = [big[:, 4608 + 512 * i:5120 + 512 * i] for i in range(2)]
        bn = wblk[:, 0:NB * 6]
        sc = Xf
        in0 = [sem(f"in0_{i}") for i in range(2)]
        z0, t_done, xT_done, adT_done, y_done, yT_done, h_done, hT_done, bn_done, adM_out = map(
            sem, ("z0", "t_done", "xT_done", "adT_done", "y_done", "yT_done", "h_done", "hT_done", "bn_done", "adM_out"))
        x_rows = x.rearrange("b n d -> (b n) d")
        with nc.Block() as block:
            @block.sync
            def _(sp):
                sp.wait_ge(z0, 1)
                for k in range(NC):
                    p = k % 2
                    if k >= 2:
                        sp.wait_ge(y_done, k - 1)
                    sp.dma_start(xin[p].rearrange("p (c d) -> p c d", d=D),
                                 x_rows[CH * k:CH * k + CH, :].rearrange("(c p) d -> p c d", p=P)).then_inc(in0[p], 16)
                    for b2 in range(2):
                        sp.dma_start(adin[p][N * b2:N * b2 + N, :].rearrange("p (c b j) -> p c b j", b=2, j=N)[:, :, b2, :],
                                     adj[8 * k:8 * k + 8].rearrange("(c b) i j -> b i c j", b=2)[b2]).then_inc(in0[p], 16)
                    for gg in range(2):
                        g0 = 8 * k + 4 * gg
                        for jh in range(JH):
                            sp.dma_start(lin[p][N * jh:N * jh + N, 128 * gg:128 * gg + 128].rearrange("p (q j) -> p q j", q=Q),
                                         adj[g0:g0 + GB].rearrange("g (t q) (h j) -> h (g t) q j", q=Q, h=JH)[jh]).then_inc(in0[p], 16)

            @block.tensor
            def _(pe):
                def turn(k):
                    p = k % 2
                    pe.wait_ge(in0[p], 112 * (k // 2 + 1))
                    if k >= 1:
                        pe.wait_ge(xT_done, k)
                        pe.wait_ge(adT_done, k)
                    for c in range(4):
                        pe.transpose(bank[0][:, 128 * c:128 * c + 128], xin[p][:, 128 * c:128 * c + 128], ident)
                        pe.transpose(bank[1][:, 128 * c:128 * c + 128], adin[p][:, 128 * c:128 * c + 128], ident)
                    for gg in range(2):
                        last = pe.transpose(bank[2][:, 128 * gg:128 * gg + 128], lin[p][:, 128 * gg:128 * gg + 128], ident)
                    last.then_inc(t_done, 1)

                def neighbours(k):
                    p = k % 2
                    pe.wait_ge(adT_done, k + 1)
                    if k >= 1:
                        pe.wait_ge(yT_done, k)
                    for c in range(4):
                        last = pe.matmul(bank[3][:, 128 * c:128 * c + 128], xin[p][:, 128 * c:128 * c + 128],
                                         adT[p][:, 128 * c:128 * c + 128], start=True, stop=True)
                    last.then_inc(y_done, 1)

                def product(k):
                    pe.wait_ge(yT_done, k + 1)
                    if k >= 1:
                        pe.wait_ge(hT_done, k)
                    pe.matmul(bank[4][:], wt["W"][:], yT[k % 2], start=True, stop=True).then_inc(h_done, 1)

                for k in range(NC + 2):
                    if k < NC:
                        turn(k)
                    if 1 <= k <= NC:
                        neighbours(k - 1)
                    if k >= 2:
                        product(k - 2)

            @block.scalar
            def _(act):
                for k in range(NC + 2):
                    if k < NC:
                        act.wait_ge(t_done, k + 1)
                        act.copy(x1T[:, CH * k:CH * k + CH], bank[0][:]).then_inc(xT_done, 1)
                    if 1 <= k <= NC:
                        act.wait_ge(y_done, k)
                        if k >= 3:
                            act.wait_ge(h_done, k - 2)
                        act.copy(yT[(k - 1) % 2], bank[3][:]).then_inc(yT_done, 1)
                    if k >= 2:
                        act.wait_ge(h_done, k - 1)
                        act.activation(hT[:, CH * (k - 2):CH * (k - 1)], bank[4][:], ACT.Identity,
                                       bias=cols[:, B0:B0 + 1]).then_inc(hT_done, 1)

            @block.vector
            def _(v):
                v.memset(adin[0], 0.0)
                v.memset(adin[1], 0.0).then_inc(z0, 1)
                for k in range(NC + 2):
                    p = k % 2
                    if k < NC:
                        v.wait_ge(t_done, k + 1)
                        if k >= 2:
                            v.wait_ge(y_done, k - 1)
                            v.wait_ge(adM_out, 16 * (k - 1))
                        v.tensor_copy(adT[p], bank[1][:])
                        v.tensor_tensor(adM[p].rearrange("p (c n) -> p c n", n=P), bank[1][:].rearrange("p (c n) -> p c n", n=P),
                                        cst[:, C_OFF:C_OFF + P].unsqueeze(1).broadcast_to([P, PAIRS, P]), ALU.mult)
                        v.tensor_tensor(wE[:, 256 * k:256 * k + 256].rearrange("p (c n) -> p c n", n=P),
                                        bank[2][:, 0:256].rearrange("p (c n) -> p c n", n=P),
                                        cst[:, C_OFFE:C_OFFE + P].unsqueeze(1).broadcast_to([P, 2, P]), ALU.mult).then_inc(adT_done, 1)
                    if k >= 2:
                        v.wait_ge(hT_done, k - 1)
                        for b in range(8 * (k - 2), 8 * (k - 1)):
                            last = v.bn_stats(bn[:, 6 * b:6 * b + 6], hT[:, N * b:N * b + N])
                        last.then_inc(bn_done, 1)

            @block.gpsimd
            def _(pool):
                for k in range(NC):
                    pool.wait_ge(adT_done, k + 1)
                    if k >= 1:
                        pool.wait_ge(adM_out, 16 * k)
                    pool.dma_start(adM_d[k], adM[k % 2]).then_inc(adM_out, 16)
                pool.wait_ge(adM_out, 16 * NC)

        a_dve, a_act, hn_done, s_done = map(sem, ("a_dve", "a_act", "hn_done", "s_done"))
        SW = 2048
        with nc.Block() as block:
            @block.vector
            def _(v):
                n = 0

                def then(ins):
                    nonlocal n
                    n += 1
                    ins.then_inc(a_dve, 1)
                    v.wait_ge(a_dve, n)
                st = bn.rearrange("p (b s) -> p b s", s=6)
                me, ve, mo, vo = (st[:, :, i] for i in (1, 2, 4, 5))
                mean, var, tmp = big[:, 0:128], big[:, 128:256], big[:, 256:384]
                scale, shift = sc[:, 0:128], sc[:, 128:256]
                then(v.tensor_tensor(mean, me, mo, ALU.add))
                then(v.tensor_tensor(tmp, me, mo, ALU.subtract))
                then(v.tensor_tensor(tmp, tmp, tmp, ALU.mult))
                then(v.tensor_tensor(var, ve, vo, ALU.add))
                then(v.tensor_scalar(var, var, 1.0 / N, None, ALU.mult))
                then(v.tensor_scalar(mean, mean, 0.5, None, ALU.mult))
                v.scalar_tensor_tensor(out=var, in0=tmp, scalar=0.25, in1=var, op0=ALU.mult, op1=ALU.add).then_inc(hn_done, 1)
                v.wait_ge(a_act, 1)
                then(v.reciprocal(scale, tmp))
                then(v.tensor_scalar(scale, scale, cols[:, GAM:GAM + 1], None, ALU.mult))
                then(v.tensor_tensor(tmp, mean, scale, ALU.mult))
                then(v.tensor_scalar(shift, tmp, -1.0, cols[:, BET:BET + 1], ALU.mult, ALU.add))
                nb = SW // N
                for k in range(NB * N // SW):
                    h = hT[:, SW * k:SW * k + SW].rearrange("p (b n) -> p b n", n=N)
                    then(v.tensor_tensor(h, h, scale[:, nb * k:nb * k + nb].unsqueeze(2).broadcast_to([P, nb, N]), ALU.mult))
                    v.tensor_tensor(h, h, shift[:, nb * k:nb * k + nb].unsqueeze(2).broadcast_to([P, nb, N]), ALU.add).then_inc(hn_done, 1)
                for k in range(NB * N // SW):
                    v.wait_ge(a_act, k + 2)
                    c = slice(SW * k, SW * k + SW)
                    v.tensor_tensor(x1T[:, c], x1T[:, c], hT[:, c], ALU.add).then_inc(s_done, 1)
                v.memset(wblk[:], 0.0)
                v.wait_ge(s_done, NB * N // SW)

            @block.scalar
            def _(act):
                act.wait_ge(hn_done, 1)
                act.activation(big[:, 256:384], big[:, 128:256], ACT.Sqrt, bias=cols[:, EPSC:EPSC + 1]).then_inc(a_act, 1)
                for k in range(NB * N // SW):
                    act.wait_ge(hn_done, k + 2)
                    c = slice(SW * k, SW * k + SW)
                    act.activation(hT[:, c], hT[:, c], ACT.Silu).then_inc(a_act, 1)

        AT = [big[:, 0 + 512 * i:512 + 512 * i] for i in range(2)]
        BT = [big[:, 1024 + 512 * i:1536 + 512 * i] for i in range(2)]
        A2 = [big[:, 2048 + 512 * i:2560 + 512 * i] for i in range(2)]
        B2 = [big[:, 3072 + 512 * i:3584 + 512 * i] for i in range(2)]
        ab_psum, ab_done, gram_done, var_done, gram_free = map(sem, ("ab_psum", "ab_done", "gram_done", "var_done", "gram_free"))
        with nc.Block() as block:
            @block.tensor
            def _(pe):
                def ab(k):
                    if k >= 1:
                        pe.wait_ge(ab_done, 4 * k)
                    pe.matmul(bank[0][:], wt["Wa"][:], x1T[:, CH * k:CH * k + CH], start=True, stop=True)
                    pe.matmul(bank[1][:], wt["Wb"][:], x1T[:, CH * k:CH * k + CH], start=True, stop=True).then_inc(ab_psum, 1)

                def gram(k):
                    p = k % 2
                    pe.wait_ge(ab_done, 4 * k + 4)
                    if k >= 2:
                        pe.wait_ge(var_done, k - 1)
                    for gg in range(2):
                        o = bank[2 + p][:, 128 * gg:128 * gg + 128]
                        view = lambda m: m[:, 256 * gg:256 * gg + 256].rearrange("p (g t q) -> p q g t", g=GB, q=Q)
                        for jh in range(JH):
                            for g in range(GB):
                                c0 = (jh * GB + g) * T
                                b0 = 256 * gg + N * g + JW * jh
                                for q in range(Q):
                                    pe.matmul(o[JW * q:JW * q + JW, c0:c0 + T], B2[p][:, b0:b0 + JW], ones[:, 0:T],
                                              start=(gg + jh + g == 0), stop=False, skip_group_check=True)
                        for q in range(Q):
                            pe.matmul(o[JW * q:JW * q + JW, :], ones[:, 0:JW],
                                      view(A2[p])[:, q].unsqueeze(1).broadcast_to([P, JH, GB, T]),
                                      start=False, stop=False, skip_group_check=True)
                        for jh in range(JH):
                            for g in range(GB):
                                for q in range(Q):
                                    c0 = (jh * GB + g) * T
                                    b0 = 256 * gg + N * g + JW * jh
                                    last = pe.matmul(o[JW * q:JW * q + JW, c0:c0 + T], BT[p][:, b0:b0 + JW],
                                                     view(AT[p])[:, q, g], start=False, stop=True, skip_group_check=True)
                    last.then_inc(gram_done, 1)

                for k in range(NC + 1):
                    if k < NC:
                        ab(k)
                    if k >= 1:
                        gram(k - 1)

            @block.scalar
            def _(act):
                for k in range(NC):
                    p = k % 2
                    act.wait_ge(ab_psum, k + 1)
                    if k >= 2:
                        act.wait_ge(gram_done, k - 1)
                    act.mul(AT[p], bank[0][:], 2.0).then_inc(ab_done, 1)
                    act.activation(A2[p], bank[0][:], ACT.Square).then_inc(ab_done, 1)
                    act.activation(BT[p], bank[1][:], ACT.Identity, bias=cols[:, BE1C:BE1C + 1]).then_inc(ab_done, 1)
                    act.activation(B2[p], bank[1][:], ACT.Square, bias=cols[:, BE1C:BE1C + 1]).then_inc(ab_done, 1)

            @block.vector
            def _(v):
                for k in range(NC):
                    v.wait_ge(gram_done, k + 1)
                    v.tensor_scalar(rE[:, 256 * k:256 * k + 256], bank[2 + k % 2][:, 0:256], 1.0 / D, 0.0,
                                    ALU.mult, ALU.max).then_inc(var_done, 1)

        sE = hT[:, 0:NG * GE]
        sq_done, st_psum, st_done, st_hi = map(sem, ("sq_done", "st_psum", "st_done", "st_hi"))
        s_out = [sem(f"s_out{i}") for i in range(2)]
        sHi, sLo = Xhi, Xlo
        with nc.Block() as block:
            @block.scalar
            def _(act):
                act.activation(sE, rE[:], ACT.Sqrt, bias=cols[:, EPSC + 1:EPSC + 2]).then_inc(sq_done, 1)
                for k in range(NG // 4):
                    act.wait_ge(st_psum, k + 1)
                    if k >= 2:
                        act.wait_ge(s_out[k % 2], 256 * (k // 2))
                    act.copy(sHi[k % 2][:], bank[k % 2][:]).then_inc(st_hi, 1)

            @block.vector
            def _(v):
                v.wait_ge(sq_done, 1)
                v.reciprocal(rE[:], sE)
                for k in range(NG // 4):
                    v.wait_ge(st_hi, k + 1)
                    v.tensor_tensor(sLo[k % 2][:], bank[k % 2][:], sHi[k % 2][:].bitcast(F32), ALU.subtract).then_inc(st_done, 1)

            @block.tensor
            def _(pe):
                pe.wait_ge(sq_done, 1)
                for k in range(NG // 4):
                    if k >= 2:
                        pe.wait_ge(st_done, k - 1)
                    for c in range(4):
                        last = pe.transpose(bank[k % 2][:, 128 * c:128 * c + 128], sE[:, 512 * k + 128 * c:512 * k + 128 * c + 128], ident)
                    last.then_inc(st_psum, 1)

            @block.sync
            def _(sp):
                for k in range(NG // 4):
                    sp.wait_ge(st_done, k + 1)
                    for part, src in enumerate((sHi[k % 2], sLo[k % 2])):
                        for c in range(4):
                            for jh in range(JH):
                                dst = s_d[part, 4 * k + c].rearrange("g (h t e) -> h g t e", h=JH, e=P)[jh]
                                sp.dma_start(dst, src[N * jh:N * jh + N, 128 * c:128 * c + 128].bitcast(F32)).then_inc(s_out[k % 2], 16)
                for p in range(2):
                    sp.wait_ge(s_out[p], 256 * (NG // 8))

        gsT = hT
        z = [big[:, 2048 * i:2048 * i + 2048] for i in range(4)]
        h_bank = [[bank[0], bank[1]], [bank[2], bank[3]]]
        psS, psX, psT = bank[4], bank[5], bank[6]
        s_in = [sem(f"s_in{i}") for i in range(2)]
        (x1s_ready, x_psum, xf_ready, x_lo, w_blk, h_ready, z_ready, g_ready, sum_done, gs_ready,
         gsT_psum, gsT_ready) = map(sem, ("x1s_ready", "x_psum", "xf_ready", "x_lo", "w_blk", "h_ready", "z_ready",
                                          "g_ready", "sum_done", "gs_ready", "gsT_psum", "gsT_ready"))
        CK = 8
        with nc.Block() as block:
            @block.sync
            def _(sp):
                def rows(g, par, n):
                    sp.wait_ge(h_ready, 2 * CK * (g - 1))
                    for c in range(4):
                        r0 = 32 * par + GB * c
                        sp.dma_start(stdR[r0:r0 + GB, :].bitcast(F32), s_d[c // 2, bass.ds(g, 1)].rearrange("o g e -> (o g) e")).then_inc(s_in[par], 16)

                def first(g, par, n):
                    for c in range(4):
                        r0 = 32 * par + GB * c
                        sp.dma_start(stdR[r0:r0 + GB, :].bitcast(F32), s_d[c // 2, g]).then_inc(s_in[par], 16)
                first(0, 0, 0)
                first(1, 1, 0)
                with sp.Fori(0, NG // 2 - 1) as i:
                    rows(i * 2 + 2, 0, i + 1)
                    rows(i * 2 + 3, 1, i + 1)

            @block.gpsimd
            def _(pool):
                def operand(g, par):
                    pool.wait_ge(x_psum, g)
                    pool.tensor_copy(x1s[:], x1T[:, bass.ds(g * (GB * N), GB * N)]).then_inc(x1s_ready, 1)
                    pool.wait_ge(x1s_ready, g + 1)

                def split(g, par):
                    pool.wait_ge(xf_ready, g + 1)
                    pool.tensor_tensor(Xlo[par][:], Xf[:], Xhi[par][:].bitcast(F32), ALU.subtract).then_inc(x_lo, 1)
                    pool.wait_ge(x_lo, g + 1)

                def weights(g, jh):
                    if not (isinstance(g, int) and g < 1):
                        pool.wait_ge(sum_done, CK * (g - 1) + CK // 2 * (jh + 1))
                    half = GB * T * 32
                    for q in range(Q):
                        src = wE[JW * q:JW * q + JW, bass.ds(g * GE + GB * T * jh, GB * T)].rearrange("p (g h t) -> p g h t", g=GB, h=2)
                        whole = wblk[JW * q:JW * q + JW, half * jh:half * jh + half]
                        dst = bass.AP(whole.tensor, whole.offset + 8 * q,
                                      [list(whole.ap[0]), [T * 32, GB], [8 * 32, 2], [33, 8]])
                        pool.tensor_copy(dst, src).then_inc(w_blk, 1)
                        pool.wait_ge(w_blk, g * (2 * Q) + (Q * jh + q + 1))

                def group(g, par, n, last=False):
                    weights(g, 0)
                    if not last:
                        operand(g + 1, 1 - par)
                        split(g + 1, 1 - par)
                    weights(g, 1)

                operand(0, 0)
                split(0, 0)
                group(0, 0, 0)
                with pool.Fori(0, NG // 2 - 1) as i:
                    group(i * 2 + 1, 1, i)
                    group(i * 2 + 2, 0, i + 1)
                group(NG - 1, 1, NG // 2 - 1, last=True)

            @block.tensor
            def _(pe):
                def operand(g):
                    pe.wait_ge(x1s_ready, g + 1)
                    pe.wait_ge(xf_ready, g)
                    for a in range(GB):
                        pe.matmul(psX[0:N, D * a:D * a + D], x1s[:, N * a:N * a + N], wt["Wag"][:],
                                  start=(a == 0), stop=True, skip_group_check=True)
                        pe.matmul(psX[N:P, D * a:D * a + D], x1s[:, N * a:N * a + N], wt["Wbg"][:],
                                  start=(a == 0), stop=False, skip_group_check=True)
                    pe.matmul(psX[N:P, :], ones[0:1, 0:N], be1row[0:1, :].unsqueeze(1).broadcast_to([1, GB, D]),
                              start=False, stop=True, skip_group_check=True).then_inc(x_psum, 1)

                def gather(g, par, c):
                    for s in range(2):
                        kk = g * (2 * CK) + (2 * c + s)
                        if not (isinstance(kk, int) and kk < 2):
                            pe.wait_ge(z_ready, kk - 1)
                        for j in range(2):
                            tile = 4 * c + 2 * s + j
                            o = h_bank[s][j][:]
                            sl = sel[:, P * tile:P * tile + P]
                            pe.matmul(o, sl, Xhi[par][:], start=True, stop=False)
                            pe.matmul(o, sl, Xlo[par][:], start=False, stop=False)
                            ins = pe.matmul(o, stdR[32 * par:32 * par + 16, P * tile:P * tile + P],
                                            bgeR[32 * par:32 * par + 16, :], start=False, stop=True)
                        ins.then_inc(h_ready, 1)

                def weigh(g, c):
                    jh = c // 4
                    pe.wait_ge(g_ready, g * CK + (c + 1))
                    if c % 4 == 0:
                        pe.wait_ge(w_blk, g * (2 * Q) + Q * (jh + 1))
                    if c == 0:
                        pe.wait_ge(gs_ready, g)
                    for j in range(4):
                        t = 4 * (c % 4) + j
                        hf = t // 8
                        for a in range(GB):
                            blk = ((jh * GB + a) * T + t) * 32
                            ins = pe.matmul(psS[32 * a:32 * a + 32, D * hf:D * hf + D], wblk[:, blk:blk + 32],
                                            z[c % 4][:, 512 * j + D * a:512 * j + D * a + D],
                                            start=(c == 0 and j == 0), stop=(jh == 1 and t % 8 == 7), skip_group_check=True)
                    ins.then_inc(sum_done, 1)

                def turn(g):
                    pe.wait_ge(gs_ready, g + 1)
                    pe.wait_ge(gsT_ready, g)
                    for hf in range(2):
                        ins = pe.transpose(psT[:, P * hf:P * hf + P], gs[:, D * hf:D * hf + D], ident)
                    ins.then_inc(gsT_psum, 1)

                def group(g, par, n, first=False, last=False):
                    pe.wait_ge(x_lo, g + 1)
                    pe.wait_ge(s_in[par], n * 64 + 64)
                    for c in range(CK):
                        gather(g, par, c)
                        if c < 2:
                            if not first:
                                weigh(g - 1, c + CK - 2)
                        else:
                            weigh(g, c - 2)
                        if c == 3 and not first:
                            turn(g - 1)
                        if c == 4 and not last:
                            operand(g + 1)

                operand(0)
                group(0, 0, 0, first=True)
                with pe.Fori(0, NG // 2 - 1) as i:
                    group(i * 2 + 1, 1, i)
                    group(i * 2 + 2, 0, i + 1)
                group(NG - 1, 1, NG // 2 - 1, last=True)
                weigh(NG - 1, CK - 2)
                weigh(NG - 1, CK - 1)
                turn(NG - 1)

            @block.vector
            def _(v):
                def group(g, par, n):
                    for c in range(CK):
                        for s in range(2):
                            kk = g * (2 * CK) + (2 * c + s)
                            v.wait_ge(h_ready, kk + 1)
                            m = g * CK + c
                            if s == 0 and not (isinstance(m, int) and m < 4):
                                v.wait_ge(sum_done, m - 3)
                            t0 = 4 * (c % 4) + 2 * s
                            r = rE[:, bass.ds(g * GE + GB * T * (c // 4), GB * T)].rearrange("p (g t) -> p t g", t=T)[:, t0:t0 + 2, :]
                            for j in range(2):
                                ins = v.tensor_tensor(z[c % 4][:, 1024 * s + 512 * j:1024 * s + 512 * j + 512].rearrange("p (g f) -> p g f", f=D),
                                                      h_bank[s][j][:].rearrange("p (g f) -> p g f", f=D),
                                                      r[:, j].unsqueeze(2).broadcast_to([P, GB, D]), ALU.mult)
                            ins.then_inc(z_ready, 1)
                steps(v, NG, group, 2, 0)

            @block.scalar
            def _(act):
                def sums(g):
                    act.wait_ge(sum_done, g * CK + CK)
                    act.wait_ge(gsT_psum, g)
                    act.copy(gs[:], psS[:, 0:2 * D]).then_inc(gs_ready, 1)

                def keep(g):
                    act.wait_ge(gsT_psum, g + 1)
                    for hf in range(2):
                        dst = gsT[:, bass.ds(g * (GB * N), GB * N)].rearrange("p (g h t q) -> p h g q t", g=GB, h=2, q=Q)[:, hf]
                        ins = act.copy(dst, psT[:, P * hf:P * hf + P].rearrange("p (g q t) -> p g q t", g=GB, q=Q))
                    ins.then_inc(gsT_ready, 1)

                def operand(g, par):
                    act.wait_ge(x_psum, g + 1)
                    act.wait_ge(x_lo, g)
                    if not (isinstance(g, int) and g < 2):
                        act.wait_ge(h_ready, 2 * CK * (g - 1))
                    act.copy(Xf[:], psX[:])
                    act.copy(Xhi[par][:], psX[:]).then_inc(xf_ready, 1)

                def group(g, par, n, first=False, last=False):
                    for c in range(CK):
                        act.wait_ge(z_ready, g * (2 * CK) + (2 * c + 2))
                        act.activation(z[c % 4], z[c % 4], ACT.Gelu).then_inc(g_ready, 1)
                        if c == 1 and not first:
                            sums(g - 1)
                        if c == 3 and not first:
                            keep(g - 1)
                        if c == 4 and not last:
                            operand(g + 1, 1 - par)

                operand(0, 0)
                group(0, 0, 0, first=True)
                with act.Fori(0, NG // 2 - 1) as i:
                    group(i * 2 + 1, 1, i)
                    group(i * 2 + 2, 0, i + 1)
                group(NG - 1, 1, NG // 2 - 1, last=True)
                sums(NG - 1)
                keep(NG - 1)

        hc = hT
        msg = stage
        adm = [big[:, 512 * i:512 * i + 512] for i in range(2)]
        sq = [big[:, 1024 + 512 * i:1536 + 512 * i] for i in range(2)]
        sd = [big[:, 2048 + 512 * i:2560 + 512 * i] for i in range(2)]
        ad_in = [sem(f"ad_in{i}") for i in range(2)]
        m_psum, m_done, n_psum, n_done, v_psum, sd_done, rr_done, u_done = map(
            sem, ("m_psum", "m_done", "n_psum", "n_done", "v_psum", "sd_done", "rr_done", "u_done"))
        with nc.Block() as block:
            @block.sync
            def _(sp):
                for k in range(NC):
                    if k >= 2:
                        sp.wait_ge(m_psum, k - 1)
                    sp.dma_start(adm[k % 2], adM_d[k]).then_inc(ad_in[k % 2], 16)

            @block.tensor
            def _(pe):
                def message(k):
                    pe.wait_ge(ad_in[k % 2], 16 * (k // 2 + 1))
                    if k >= 1:
                        pe.wait_ge(m_done, k)
                    pe.matmul(bank[0][:], wt["We2"][:], gsT[:, CH * k:CH * k + CH], start=True, stop=False)
                    pe.matmul(bank[0][:], be2_b[:], adm[k % 2], start=False, stop=True).then_inc(m_psum, 1)

                def hidden(k):
                    pe.wait_ge(m_done, k + 1)
                    if k >= 1:
                        pe.wait_ge(n_done, 2 * k)
                    pe.matmul(bank[1][:], wt["Wna"][:], x1T[:, CH * k:CH * k + CH], start=True, stop=False)
                    pe.matmul(bank[1][:], wt["Wnb"][:], msg[k % 2][:], start=False, stop=True).then_inc(n_psum, 1)

                def variance(k):
                    pe.wait_ge(n_done, 2 * k + 2)
                    if k >= 1:
                        pe.wait_ge(sd_done, k)
                    pe.matmul(bank[2][:], ones[:], sq[k % 2], start=True, stop=True).then_inc(v_psum, 1)

                for k in range(NC + 2):
                    if k < NC:
                        message(k)
                    if 1 <= k <= NC:
                        hidden(k - 1)
                    if k >= 2:
                        variance(k - 2)

            @block.scalar
            def _(act):
                for k in range(NC + 2):
                    if k < NC:
                        act.wait_ge(m_psum, k + 1)
                        if k >= 2:
                            act.wait_ge(n_psum, k - 1)
                        act.copy(msg[k % 2][:], bank[0][:]).then_inc(m_done, 1)
                    if 1 <= k <= NC:
                        c = slice(CH * (k - 1), CH * k)
                        act.wait_ge(n_psum, k)
                        if k >= 3:
                            act.wait_ge(v_psum, k - 2)
                        act.activation(hc[:, c], bank[1][:], ACT.Identity, bias=cols[:, BN1C:BN1C + 1]).then_inc(n_done, 1)
                        act.activation(sq[(k - 1) % 2], bank[1][:], ACT.Square, bias=cols[:, BN1C:BN1C + 1]).then_inc(n_done, 1)
                    if k >= 2:
                        act.wait_ge(v_psum, k - 1)
                        if k >= 4:
                            act.wait_ge(u_done, k - 3)
                        act.activation(sd[k % 2], bank[2][:], ACT.Sqrt, scale=1.0 / D, bias=cols[:, EPSC + 1:EPSC + 2]).then_inc(sd_done, 1)

            @block.vector
            def _(v):
                for k in range(NC):
                    c = slice(CH * k, CH * k + CH)
                    v.wait_ge(sd_done, k + 1)
                    v.reciprocal(sd[k % 2], sd[k % 2]).then_inc(rr_done, 1)
                    v.wait_ge(rr_done, k + 1)
                    v.wait_ge(n_done, 2 * k + 2)
                    v.tensor_tensor(hc[:, c], hc[:, c], sd[k % 2], ALU.mult).then_inc(u_done, 1)

        g2 = [big[:, 512 * i:512 * i + 512] for i in range(2)]
        ob = [big[:, 1024 + 512 * i:1536 + 512 * i] for i in range(2)]
        xs = [big[:, 2048 + 512 * i:2560 + 512 * i] for i in range(2)]
        g2_done, o_psum, o_done = map(sem, ("g2_done", "o_psum", "o_done"))
        o_out = [sem(f"o_out{i}") for i in range(2)]
        out_rows = out.rearrange("b n d -> (b n) d")
        with nc.Block() as block:
            @block.scalar
            def _(act):
                for k in range(NC):
                    if k >= 2:
                        act.wait_ge(o_psum, k - 1)
                    act.activation(g2[k % 2], hc[:, CH * k:CH * k + CH], ACT.Gelu, scale=cols[:, GN:GN + 1],
                                   bias=cols[:, BGN:BGN + 1]).then_inc(g2_done, 1)

            @block.tensor
            def _(pe):
                for k in range(NC):
                    pe.wait_ge(g2_done, k + 1)
                    if k >= 2:
                        pe.wait_ge(o_done, k - 1)
                    o = bank[k % 2]
                    for c in range(PAIRS):
                        r = slice(P * c, P * c + P)
                        pe.matmul(o[:, r], g2[k % 2][:, r], wt["Wn2"][:], start=(c == 0), stop=False, skip_group_check=True)
                        pe.matmul(o[:, r], x1T[:, CH * k + P * c:CH * k + P * c + P], ident, start=False, stop=False, skip_group_check=True)
                        ins = pe.matmul(o[:, r], ones[0:1, :], bn2row[0:1, :], start=False, stop=True, skip_group_check=True)
                    ins.then_inc(o_psum, 1)

            @block.vector
            def _(v):
                for k in range(NC):
                    v.wait_ge(o_psum, k + 1)
                    if k >= 2:
                        v.wait_ge(o_out[k % 2], 16 * (k // 2))
                    v.tensor_copy(ob[k % 2], bank[k % 2][:]).then_inc(o_done, 1)

            @block.sync
            def _(sp):
                for k in range(NC):
                    sp.wait_ge(o_done, k + 1)
                    sp.dma_start(out_rows[CH * k:CH * k + CH, :].rearrange("(c p) d -> p c d", p=P),
                                 ob[k % 2].rearrange("p (c d) -> p c d", d=D)).then_inc(o_out[k % 2], 16)
                for p in range(2):
                    sp.wait_ge(o_out[p], 16 * (NC // 2))


NAMES = ["L0_gnn_W", "L0_gnn_b", "L0_gnn_gamma", "L0_gnn_beta", "L1_gnn_We1", "L1_gnn_be1", "L1_gnn_ge", "L1_gnn_bge",
         "L1_gnn_We2", "L1_gnn_be2", "L1_gnn_Wn1", "L1_gnn_bn1", "L1_gnn_gn", "L1_gnn_bgn", "L1_gnn_Wn2", "L1_gnn_bn2"]


def kernel(**inputs):
    import concourse.bacc as bacc
    from concourse.bass_utils import run_bass_kernel_spmd

    nc = bacc.Bacc("TRN2", target_bir_lowering=False, num_devices=1)
    arrays = {f"in_{n}": np.ascontiguousarray(inputs[n]) for n in ["x", "adj"] + NAMES}
    arrays["in_consts"] = constants()
    ap = {n: nc.dram_tensor(n, a.shape, mybir.dt.from_np(a.dtype), kind="ExternalInput").ap() for n, a in arrays.items()}
    out = nc.dram_tensor("out", (NB, N, D), F32, kind="ExternalOutput").ap()
    build(nc, ap["in_x"], ap["in_adj"], ap["in_consts"], {n: ap[f"in_{n}"] for n in NAMES}, out)
    r = run_bass_kernel_spmd(nc, [arrays], core_ids=[0])
    return r.results[0]["out"]
```

```python
from contextlib import ExitStack

import numpy as np

import concourse.bass as bass
from concourse import mybir

F32 = mybir.dt.float32
F32R = mybir.dt.float32r
ACT = mybir.ActivationFunctionType
ALU = mybir.AluOpType
AX = mybir.AxisListType

P = 128
NB = 128
N = 64
D = 128
GB = 4
NG = NB // GB
JH = 2
JW = N // JH
Q = P // JW
T = N // Q
GE = JH * GB * T
CH = 512
NC = NB * N // CH
PAIRS = CH // P
EPS0, EPS1 = 1e-3, 1e-5

C_ID, C_OFF, C_OFFE, C_CEN, C_BM, C_SEL = 0, 128, 256, 384, 512, 520
C_ALL = C_SEL + T * P

TB = 4
AW = N // TB
R_B, R_A, R_S, R_END = 0, 2 * JW, 2 * JW + 2 * AW, 2 * JW + 2 * AW + 4 * GB
CHUNKS = [(0, 3), (3, 3), (6, 3), (9, 3), (12, 2), (14, 2)]
CK = len(CHUNKS) * JH
LAG = 3
OPERAND, TURN = 1, 5


def constants():
    c = np.zeros((P, C_ALL), np.float32)
    eye = np.eye(P, dtype=np.float32)
    c[:, C_ID:C_ID + P] = eye
    c[:, C_OFF:C_OFF + P] = 1 - eye
    c[:, C_CEN:C_CEN + P] = eye - 1.0 / D
    e = np.arange(P)
    q, jj = e // JW, e % JW
    for jh in range(JH):
        for g in range(GB):
            for t in range(T):
                c[:, C_OFFE + (jh * GB + g) * T + t] = Q * t + q != JW * jh + jj
    for part in range(4):
        for g in range(GB):
            c[R_S + GB * part + g, C_BM + 4 * (part % 2) + g] = 1
    sel = c[:, C_SEL:].reshape(P, T, P)
    for t in range(T):
        for lo in (0, 1):
            sel[R_B + 2 * jj + lo, t, e] = 1
            sel[R_A + 2 * (Q * (t % (T // TB)) + q) + lo, t, e] = 1
    return c


def steps(eng, n, body, head, tail):
    assert head % 2 == 0 and (n - head - tail) % 2 == 0
    for k in range(head):
        body(k, k % 2, k // 2)
    with eng.Fori(0, (n - head - tail) // 2) as i:
        body(i * 2 + head, 0, i + head // 2)
        body(i * 2 + head + 1, 1, i + head // 2)
    for k in range(n - tail, n):
        body(k, k % 2, k // 2)


def build(nc, x, adj, consts, w, out):
    with ExitStack() as ctx:
        def sb(name, shape, dt=F32):
            return ctx.enter_context(nc.sbuf_tensor(name, shape, dt))

        def sem(name):
            return ctx.enter_context(nc.semaphore(name))

        psum = ctx.enter_context(nc.psum_tensor("psum", [P, 8 * 512], F32))
        bank = [psum[:, 512 * i:512 * i + 512] for i in range(8)]

        x1T = sb("x1T", [P, NB * N])
        hT = sb("hT", [P, NB * N])
        wE = sb("wE", [P, NG * GE])
        rE = sb("rE", [P, NG * GE])
        cst = sb("cst", [P, C_SEL])
        wt = {n: sb(n, [P, D]) for n in ("W", "Wa", "Wb", "We2", "Wna", "Wnb", "Wn2", "Wag", "Wbg")}
        ge_b = sb("ge_b", [P, D])
        bge_b = sb("bge_b", [P, D])
        be2_b = sb("be2_b", [P, D])
        cols = sb("cols", [P, 16])
        B0, GAM, BET, BE1, BN1, GN, BGN, BE1C, BN1C, EPSC, MEAN4 = 0, 1, 2, 3, 4, 5, 6, 7, 8, 9, 11
        bn2row = sb("bn2row", [1, D])
        be1row = sb("be1row", [1, D])
        ones = sb("ones", [P, D])
        ident = cst[:, C_ID:C_ID + P]
        pick = [sb(f"pick{i}", [P, T * P], F32R) for i in range(JH)]
        nodes = [sb(f"nodes{i}", [P, TB * GB * D], F32R) for i in range(JH)]
        big = sb("big", [P, 4 * 1536])
        wblk = sb("wblk", [P, JH * GB * T * 32])
        Xf = sb("Xf", [P, GB * D])
        X2 = [sb(f"X2_{i}", [P, 2 * GB * D], F32R) for i in range(2)]
        Xhi = [x2[:, 0:GB * D] for x2 in X2]
        Xlo = [x2[:, GB * D:2 * GB * D] for x2 in X2]
        x1s = sb("x1s", [P, GB * N])
        gs = sb("gs", [P, 2 * D])
        stage = [sb(f"stage{i}", [P, CH]) for i in range(2)]

        adM_d = nc.dram_tensor("adM_d", [NC, P, CH], F32, kind="Internal").ap()
        s_d = nc.dram_tensor("s_d", [NG, JH, 4, GB * T, P], F32, kind="Internal").ap()
        x_d = nc.dram_tensor("x_d", [NG, 2 * P, GB * D], F32, kind="Internal").ap()

        w_in, w_ready, w_psum, w_cols, w_row, w_done = map(sem, ("w_in", "w_ready", "w_psum", "w_cols", "w_row", "w_done"))
        col_of = {"L0_gnn_b": B0, "L0_gnn_gamma": GAM, "L0_gnn_beta": BET, "L1_gnn_be1": BE1,
                  "L1_gnn_bn1": BN1, "L1_gnn_gn": GN, "L1_gnn_bgn": BGN}
        with nc.Block() as block:
            @block.sync
            def _(sp):
                n = 0
                for dst, src in ([(cst[:], consts[:, 0:C_SEL]), (big[:, 0:T * P], consts[:, C_SEL:C_ALL]),
                                  (wt["W"][:], w["L0_gnn_W"]), (wt["Wa"][:], w["L1_gnn_We1"][0:D, :]),
                                  (wt["Wb"][:], w["L1_gnn_We1"][D:2 * D, :]), (wt["We2"][:], w["L1_gnn_We2"]),
                                  (wt["Wna"][:], w["L1_gnn_Wn1"][0:D, :]), (wt["Wnb"][:], w["L1_gnn_Wn1"][D:2 * D, :]),
                                  (wt["Wn2"][:], w["L1_gnn_Wn2"]),
                                  (ge_b[:], w["L1_gnn_ge"].partition_broadcast(P)),
                                  (bge_b[:], w["L1_gnn_bge"].partition_broadcast(P)),
                                  (be2_b[:], w["L1_gnn_be2"].partition_broadcast(P)),
                                  (bn2row[:], w["L1_gnn_bn2"].unsqueeze(0))]
                                 + [(cols[:, c:c + 1], w[name].unsqueeze(1)) for name, c in col_of.items()]):
                    sp.dma_start(dst, src).then_inc(w_in, 16)
                    n += 16
                assert n == 16 * 20

            @block.tensor
            def _(pe):
                pe.wait_ge(w_in, 320)
                pe.matmul(bank[0][:, 0:2], cst[:, C_CEN:C_CEN + P], cols[:, BE1:BE1 + 2], start=True, stop=True).then_inc(w_psum, 1)
                pe.wait_ge(w_cols, 1)
                pe.matmul(bank[1][0:1, 0:D], cols[:, BE1C:BE1C + 1], ident, start=True, stop=True).then_inc(w_psum, 1)

            @block.scalar
            def _(act):
                act.wait_ge(w_in, 320)
                for jh in range(JH):
                    act.copy(pick[jh][0:R_S, :], big[0:R_S, 0:T * P]).then_inc(w_done, 1)

            @block.vector
            def _(v):
                v.memset(ones[:], 1.0)
                v.memset(wblk[:], 0.0)
                v.memset(cols[:, EPSC:EPSC + 1], EPS0)
                v.memset(cols[:, EPSC + 1:EPSC + 2], EPS1).then_inc(w_ready, 1)
                v.wait_ge(w_in, 320)
                r = 1
                for i, name in enumerate(("Wa", "Wb", "Wna", "Wnb")):
                    m = cols[:, MEAN4 + i:MEAN4 + i + 1]
                    v.tensor_reduce(m, wt[name][:], AX.X, ALU.add).then_inc(w_ready, 1)
                    v.wait_ge(w_ready, r + 1)
                    v.tensor_scalar(m, m, 1.0 / D, None, ALU.mult).then_inc(w_ready, 1)
                    v.wait_ge(w_ready, r + 2)
                    v.tensor_scalar(wt[name][:], wt[name][:], m, None, ALU.subtract).then_inc(w_ready, 1)
                    r += 3
                v.wait_ge(w_ready, r)
                v.tensor_tensor(wt["Wag"][:], wt["Wa"][:], ge_b[:], ALU.mult)
                v.tensor_tensor(wt["Wbg"][:], wt["Wb"][:], ge_b[:], ALU.mult)
                v.wait_ge(w_psum, 1)
                v.tensor_copy(cols[:, BE1C:BE1C + 2], bank[0][:, 0:2]).then_inc(w_cols, 1)
                v.wait_ge(w_psum, 2)
                v.tensor_tensor(be1row[:], bank[1][0:1, 0:D], ge_b[0:1, :], ALU.mult)
                rows = slice(R_S, R_END)
                hi, lo, hi_g = big[rows, 5000:5000 + D], big[rows, 5200:5200 + D], big[rows, 5400:5400 + GB * D]
                v.tensor_copy(nodes[0][rows, 0:D], bge_b[rows, :]).then_inc(w_row, 1)
                v.wait_ge(w_row, 1)
                v.tensor_copy(hi, nodes[0][rows, 0:D].bitcast(F32)).then_inc(w_row, 1)
                v.wait_ge(w_row, 2)
                v.tensor_tensor(lo, bge_b[rows, :], hi, ALU.subtract).then_inc(w_row, 1)
                for g in range(GB):
                    v.tensor_scalar(hi_g[:, D * g:D * g + D], hi, cst[rows, C_BM + g:C_BM + g + 1], None, ALU.mult).then_inc(w_row, 1)
                v.wait_ge(w_row, 3 + GB)
                for jh in range(JH):
                    for tb in range(TB):
                        for g in range(GB):
                            c0 = (tb * GB + g) * D
                            v.scalar_tensor_tensor(out=nodes[jh][rows, c0:c0 + D], in0=lo,
                                                   scalar=cst[rows, C_BM + 4 + g:C_BM + 5 + g],
                                                   in1=hi_g[:, D * g:D * g + D], op0=ALU.mult, op1=ALU.add)

        xin = [big[:, 0 + 512 * i:512 + 512 * i] for i in range(2)]
        adin = [big[:, 1024 + 512 * i:1536 + 512 * i] for i in range(2)]
        lin = [big[:, 2048 + 256 * i:2304 + 256 * i] for i in range(2)]
        adT = [big[:, 2560 + 512 * i:3072 + 512 * i] for i in range(2)]
        adM = [big[:, 3584 + 512 * i:4096 + 512 * i] for i in range(2)]
        yT = [big[:, 4608 + 512 * i:5120 + 512 * i] for i in range(2)]
        bn = wblk[:, 0:NB * 6]
        sc = Xf
        in0 = [sem(f"in0_{i}") for i in range(2)]
        z0, t_done, xT_done, adT_done, y_done, yT_done, h_done, hT_done, bn_done, adM_out = map(
            sem, ("z0", "t_done", "xT_done", "adT_done", "y_done", "yT_done", "h_done", "hT_done", "bn_done", "adM_out"))
        x_rows = x.rearrange("b n d -> (b n) d")
        with nc.Block() as block:
            @block.sync
            def _(sp):
                sp.wait_ge(z0, 1)
                for k in range(NC):
                    p = k % 2
                    if k >= 2:
                        sp.wait_ge(y_done, k - 1)
                    sp.dma_start(xin[p].rearrange("p (c d) -> p c d", d=D),
                                 x_rows[CH * k:CH * k + CH, :].rearrange("(c p) d -> p c d", p=P)).then_inc(in0[p], 16)
                    for b2 in range(2):
                        sp.dma_start(adin[p][N * b2:N * b2 + N, :].rearrange("p (c b j) -> p c b j", b=2, j=N)[:, :, b2, :],
                                     adj[8 * k:8 * k + 8].rearrange("(c b) i j -> b i c j", b=2)[b2]).then_inc(in0[p], 16)
                    for gg in range(2):
                        g0 = 8 * k + 4 * gg
                        for jh in range(JH):
                            sp.dma_start(lin[p][N * jh:N * jh + N, 128 * gg:128 * gg + 128].rearrange("p (q j) -> p q j", q=Q),
                                         adj[g0:g0 + GB].rearrange("g (t q) (h j) -> h (g t) q j", q=Q, h=JH)[jh]).then_inc(in0[p], 16)

            @block.tensor
            def _(pe):
                def turn(k):
                    p = k % 2
                    pe.wait_ge(in0[p], 112 * (k // 2 + 1))
                    if k >= 1:
                        pe.wait_ge(xT_done, k)
                        pe.wait_ge(adT_done, k)
                    for c in range(4):
                        pe.transpose(bank[0][:, 128 * c:128 * c + 128], xin[p][:, 128 * c:128 * c + 128], ident)
                        pe.transpose(bank[1][:, 128 * c:128 * c + 128], adin[p][:, 128 * c:128 * c + 128], ident)
                    for gg in range(2):
                        last = pe.transpose(bank[2][:, 128 * gg:128 * gg + 128], lin[p][:, 128 * gg:128 * gg + 128], ident)
                    last.then_inc(t_done, 1)

                def neighbours(k):
                    p = k % 2
                    pe.wait_ge(adT_done, k + 1)
                    if k >= 1:
                        pe.wait_ge(yT_done, k)
                    for c in range(4):
                        last = pe.matmul(bank[3][:, 128 * c:128 * c + 128], xin[p][:, 128 * c:128 * c + 128],
                                         adT[p][:, 128 * c:128 * c + 128], start=True, stop=True)
                    last.then_inc(y_done, 1)

                def product(k):
                    pe.wait_ge(yT_done, k + 1)
                    if k >= 1:
                        pe.wait_ge(hT_done, k)
                    pe.matmul(bank[4][:], wt["W"][:], yT[k % 2], start=True, stop=True).then_inc(h_done, 1)

                for k in range(NC + 2):
                    if k < NC:
                        turn(k)
                    if 1 <= k <= NC:
                        neighbours(k - 1)
                    if k >= 2:
                        product(k - 2)

            @block.scalar
            def _(act):
                for k in range(NC + 2):
                    if k < NC:
                        act.wait_ge(t_done, k + 1)
                        act.copy(x1T[:, CH * k:CH * k + CH], bank[0][:]).then_inc(xT_done, 1)
                    if 1 <= k <= NC:
                        act.wait_ge(y_done, k)
                        if k >= 3:
                            act.wait_ge(h_done, k - 2)
                        act.copy(yT[(k - 1) % 2], bank[3][:]).then_inc(yT_done, 1)
                    if k >= 2:
                        act.wait_ge(h_done, k - 1)
                        act.activation(hT[:, CH * (k - 2):CH * (k - 1)], bank[4][:], ACT.Identity,
                                       bias=cols[:, B0:B0 + 1]).then_inc(hT_done, 1)

            @block.vector
            def _(v):
                v.memset(adin[0], 0.0)
                v.memset(adin[1], 0.0).then_inc(z0, 1)
                for k in range(NC + 2):
                    p = k % 2
                    if k < NC:
                        v.wait_ge(t_done, k + 1)
                        if k >= 2:
                            v.wait_ge(y_done, k - 1)
                            v.wait_ge(adM_out, 16 * (k - 1))
                        v.tensor_copy(adT[p], bank[1][:])
                        v.tensor_tensor(adM[p].rearrange("p (c n) -> p c n", n=P), bank[1][:].rearrange("p (c n) -> p c n", n=P),
                                        cst[:, C_OFF:C_OFF + P].unsqueeze(1).broadcast_to([P, PAIRS, P]), ALU.mult)
                        v.tensor_tensor(wE[:, 256 * k:256 * k + 256].rearrange("p (c n) -> p c n", n=P),
                                        bank[2][:, 0:256].rearrange("p (c n) -> p c n", n=P),
                                        cst[:, C_OFFE:C_OFFE + P].unsqueeze(1).broadcast_to([P, 2, P]), ALU.mult).then_inc(adT_done, 1)
                    if k >= 2:
                        v.wait_ge(hT_done, k - 1)
                        for b in range(8 * (k - 2), 8 * (k - 1)):
                            last = v.bn_stats(bn[:, 6 * b:6 * b + 6], hT[:, N * b:N * b + N])
                        last.then_inc(bn_done, 1)

            @block.gpsimd
            def _(pool):
                for k in range(NC):
                    pool.wait_ge(adT_done, k + 1)
                    if k >= 1:
                        pool.wait_ge(adM_out, 16 * k)
                    pool.dma_start(adM_d[k], adM[k % 2]).then_inc(adM_out, 16)
                pool.wait_ge(adM_out, 16 * NC)

        a_dve, a_act, hn_done, s_done = map(sem, ("a_dve", "a_act", "hn_done", "s_done"))
        SW = 2048
        with nc.Block() as block:
            @block.vector
            def _(v):
                n = 0

                def then(ins):
                    nonlocal n
                    n += 1
                    ins.then_inc(a_dve, 1)
                    v.wait_ge(a_dve, n)
                st = bn.rearrange("p (b s) -> p b s", s=6)
                me, ve, mo, vo = (st[:, :, i] for i in (1, 2, 4, 5))
                mean, var, tmp = big[:, 0:128], big[:, 128:256], big[:, 256:384]
                scale, shift = sc[:, 0:128], sc[:, 128:256]
                then(v.tensor_tensor(mean, me, mo, ALU.add))
                then(v.tensor_tensor(tmp, me, mo, ALU.subtract))
                then(v.tensor_tensor(tmp, tmp, tmp, ALU.mult))
                then(v.tensor_tensor(var, ve, vo, ALU.add))
                then(v.tensor_scalar(var, var, 1.0 / N, None, ALU.mult))
                then(v.tensor_scalar(mean, mean, 0.5, None, ALU.mult))
                v.scalar_tensor_tensor(out=var, in0=tmp, scalar=0.25, in1=var, op0=ALU.mult, op1=ALU.add).then_inc(hn_done, 1)
                v.wait_ge(a_act, 1)
                then(v.reciprocal(scale, tmp))
                then(v.tensor_scalar(scale, scale, cols[:, GAM:GAM + 1], None, ALU.mult))
                then(v.tensor_tensor(tmp, mean, scale, ALU.mult))
                then(v.tensor_scalar(shift, tmp, -1.0, cols[:, BET:BET + 1], ALU.mult, ALU.add))
                nb = SW // N
                for k in range(NB * N // SW):
                    h = hT[:, SW * k:SW * k + SW].rearrange("p (b n) -> p b n", n=N)
                    then(v.tensor_tensor(h, h, scale[:, nb * k:nb * k + nb].unsqueeze(2).broadcast_to([P, nb, N]), ALU.mult))
                    v.tensor_tensor(h, h, shift[:, nb * k:nb * k + nb].unsqueeze(2).broadcast_to([P, nb, N]), ALU.add).then_inc(hn_done, 1)
                for k in range(NB * N // SW):
                    v.wait_ge(a_act, k + 2)
                    c = slice(SW * k, SW * k + SW)
                    v.tensor_tensor(x1T[:, c], x1T[:, c], hT[:, c], ALU.add).then_inc(s_done, 1)
                v.memset(wblk[:], 0.0)
                v.wait_ge(s_done, NB * N // SW)

            @block.scalar
            def _(act):
                act.wait_ge(hn_done, 1)
                act.activation(big[:, 256:384], big[:, 128:256], ACT.Sqrt, bias=cols[:, EPSC:EPSC + 1]).then_inc(a_act, 1)
                for k in range(NB * N // SW):
                    act.wait_ge(hn_done, k + 2)
                    c = slice(SW * k, SW * k + SW)
                    act.activation(hT[:, c], hT[:, c], ACT.Silu).then_inc(a_act, 1)

        AT = [big[:, 0 + 512 * i:512 + 512 * i] for i in range(2)]
        BT = [big[:, 1024 + 512 * i:1536 + 512 * i] for i in range(2)]
        A2 = [big[:, 2048 + 512 * i:2560 + 512 * i] for i in range(2)]
        B2 = [big[:, 3072 + 512 * i:3584 + 512 * i] for i in range(2)]
        ab_psum, ab_done, gram_done, var_done, gram_free = map(sem, ("ab_psum", "ab_done", "gram_done", "var_done", "gram_free"))
        with nc.Block() as block:
            @block.tensor
            def _(pe):
                def ab(k):
                    if k >= 1:
                        pe.wait_ge(ab_done, 4 * k)
                    pe.matmul(bank[0][:], wt["Wa"][:], x1T[:, CH * k:CH * k + CH], start=True, stop=True)
                    pe.matmul(bank[1][:], wt["Wb"][:], x1T[:, CH * k:CH * k + CH], start=True, stop=True).then_inc(ab_psum, 1)

                def gram(k):
                    p = k % 2
                    pe.wait_ge(ab_done, 4 * k + 4)
                    if k >= 2:
                        pe.wait_ge(var_done, k - 1)
                    for gg in range(2):
                        o = bank[2 + p][:, 128 * gg:128 * gg + 128]
                        view = lambda m: m[:, 256 * gg:256 * gg + 256].rearrange("p (g t q) -> p q g t", g=GB, q=Q)
                        for jh in range(JH):
                            for g in range(GB):
                                c0 = (jh * GB + g) * T
                                b0 = 256 * gg + N * g + JW * jh
                                for q in range(Q):
                                    pe.matmul(o[JW * q:JW * q + JW, c0:c0 + T], B2[p][:, b0:b0 + JW], ones[:, 0:T],
                                              start=(gg + jh + g == 0), stop=False, skip_group_check=True)
                        for q in range(Q):
                            pe.matmul(o[JW * q:JW * q + JW, :], ones[:, 0:JW],
                                      view(A2[p])[:, q].unsqueeze(1).broadcast_to([P, JH, GB, T]),
                                      start=False, stop=False, skip_group_check=True)
                        for jh in range(JH):
                            for g in range(GB):
                                for q in range(Q):
                                    c0 = (jh * GB + g) * T
                                    b0 = 256 * gg + N * g + JW * jh
                                    last = pe.matmul(o[JW * q:JW * q + JW, c0:c0 + T], BT[p][:, b0:b0 + JW],
                                                     view(AT[p])[:, q, g], start=False, stop=True, skip_group_check=True)
                    last.then_inc(gram_done, 1)

                for k in range(NC + 1):
                    if k < NC:
                        ab(k)
                    if k >= 1:
                        gram(k - 1)

            @block.scalar
            def _(act):
                for k in range(NC):
                    p = k % 2
                    act.wait_ge(ab_psum, k + 1)
                    if k >= 2:
                        act.wait_ge(gram_done, k - 1)
                    act.mul(AT[p], bank[0][:], 2.0).then_inc(ab_done, 1)
                    act.activation(A2[p], bank[0][:], ACT.Square).then_inc(ab_done, 1)
                    act.activation(BT[p], bank[1][:], ACT.Identity, bias=cols[:, BE1C:BE1C + 1]).then_inc(ab_done, 1)
                    act.activation(B2[p], bank[1][:], ACT.Square, bias=cols[:, BE1C:BE1C + 1]).then_inc(ab_done, 1)

            @block.vector
            def _(v):
                for k in range(NC):
                    v.wait_ge(gram_done, k + 1)
                    v.tensor_scalar(rE[:, 256 * k:256 * k + 256], bank[2 + k % 2][:, 0:256], 1.0 / D, 0.0,
                                    ALU.mult, ALU.max).then_inc(var_done, 1)

        sE = hT[:, 0:NG * GE]
        sq_done, st_psum, st_done, st_hi = map(sem, ("sq_done", "st_psum", "st_done", "st_hi"))
        s_out = [sem(f"s_out{i}") for i in range(2)]
        sHi, sLo = Xhi, Xlo
        with nc.Block() as block:
            @block.scalar
            def _(act):
                act.activation(sE, rE[:], ACT.Sqrt, bias=cols[:, EPSC + 1:EPSC + 2]).then_inc(sq_done, 1)
                for k in range(NG // 4):
                    act.wait_ge(st_psum, k + 1)
                    if k >= 2:
                        act.wait_ge(s_out[k % 2], 128 * (k // 2))
                    act.copy(sHi[k % 2], bank[k % 2][:]).then_inc(st_hi, 1)

            @block.vector
            def _(v):
                v.wait_ge(sq_done, 1)
                v.reciprocal(rE[:], sE)
                for k in range(NG // 4):
                    v.wait_ge(st_hi, k + 1)
                    v.tensor_tensor(sLo[k % 2], bank[k % 2][:], sHi[k % 2].bitcast(F32), ALU.subtract).then_inc(st_done, 1)

            @block.tensor
            def _(pe):
                pe.wait_ge(sq_done, 1)
                for k in range(NG // 4):
                    if k >= 2:
                        pe.wait_ge(st_done, k - 1)
                    for c in range(4):
                        last = pe.transpose(bank[k % 2][:, 128 * c:128 * c + 128], sE[:, 512 * k + 128 * c:512 * k + 128 * c + 128], ident)
                    last.then_inc(st_psum, 1)

            @block.sync
            def _(sp):
                for k in range(NG // 4):
                    sp.wait_ge(st_done, k + 1)
                    for part, src in enumerate((sHi[k % 2], sLo[k % 2])):
                        for jh in range(JH):
                            rows = src[GB * T * jh:GB * T * (jh + 1), :].bitcast(F32).rearrange("p (c e) -> p c e", e=P)
                            for twice in range(2):
                                sp.dma_start(s_d[4 * k:4 * k + 4, jh, 2 * part + twice].rearrange("c r e -> r c e"),
                                             rows).then_inc(s_out[k % 2], 16)
                for p in range(2):
                    sp.wait_ge(s_out[p], 128 * (NG // 8))

        gsT = hT
        z = [big[:, 1536 * i:1536 * i + 1536] for i in range(4)]
        hbuf = [psum[:, 1536 * i:1536 * i + 1536] for i in range(2)]
        psS, psX, psT = bank[6], bank[7], bank[7]
        op_in = [sem(f"op_in{i}") for i in range(JH)]
        x_out = sem("x_out")
        (x1s_ready, x_psum, xf_ready, x_lo, w_blk, h_ready, z_ready, g_ready, sum_done, gs_ready,
         gsT_psum, gsT_ready) = map(sem, ("x1s_ready", "x_psum", "xf_ready", "x_lo", "w_blk", "h_ready", "z_ready",
                                          "g_ready", "sum_done", "gs_ready", "gsT_psum", "gsT_ready"))

        def chunk(c):
            return (c // len(CHUNKS),) + CHUNKS[c % len(CHUNKS)]

        with nc.Block() as block:
            @block.sync
            def _(sp):
                def load(g, par):
                    sp.wait_ge(x_lo, g + 1)
                    sp.dma_start(x_d[bass.ds(g, 1)].rearrange("o (p h) n -> (o p) h n", h=2),
                                 X2[par][:].bitcast(F32).rearrange("p (h n) -> p h n", h=2)).then_inc(x_out, 16)
                    sp.wait_ge(x_out, g * 16 + 16)
                    for jh in range(JH):
                        if not (isinstance(g, int) and g < 1):
                            sp.wait_ge(h_ready, g * CK + (CK // JH * (jh + 1) - CK))
                        b0 = P + 2 * JW * jh
                        sp.dma_start(nodes[jh][R_B:R_A, :].bitcast(F32).rearrange("p (b n) -> p b n", b=TB),
                                     x_d[bass.ds(g, 1), b0:b0 + 2 * JW].rearrange("o p n -> (o p) n")
                                     .unsqueeze(1).broadcast_to([2 * JW, TB, GB * D])).then_inc(op_in[jh], 16)
                        sp.dma_start(nodes[jh][R_A:R_S, :].bitcast(F32).rearrange("p (b n) -> p b n", b=TB),
                                     x_d[bass.ds(g, 1), 0:P].rearrange("o (b p) n -> (o p) b n", b=TB)).then_inc(op_in[jh], 16)
                        sp.dma_start(pick[jh][R_S:R_END, :].bitcast(F32),
                                     s_d[bass.ds(g, 1), jh].rearrange("o c (g t) e -> (o c g) (t e)", g=GB)).then_inc(op_in[jh], 16)
                load(0, 0)
                load(1, 1)
                with sp.Fori(0, NG // 2 - 1) as i:
                    load(i * 2 + 2, 0)
                    load(i * 2 + 3, 1)

            LOADS = 3 * 16

            @block.gpsimd
            def _(pool):
                def operand(g):
                    pool.wait_ge(x_psum, g)
                    pool.tensor_copy(x1s[:], x1T[:, bass.ds(g * (GB * N), GB * N)]).then_inc(x1s_ready, 1)
                    pool.wait_ge(x1s_ready, g + 1)

                def split(g, par):
                    pool.wait_ge(xf_ready, g + 1)
                    pool.tensor_tensor(Xlo[par], Xf[:], Xhi[par].bitcast(F32), ALU.subtract).then_inc(x_lo, 1)
                    pool.wait_ge(x_lo, g + 1)

                def weights(g, jh):
                    if not (isinstance(g, int) and g < 1):
                        pool.wait_ge(sum_done, g * CK + (CK // JH * (jh + 1) - CK))
                    half = GB * T * 32
                    for q in range(Q):
                        src = wE[JW * q:JW * q + JW, bass.ds(g * GE + GB * T * jh, GB * T)].rearrange("p (g h t) -> p g h t", g=GB, h=2)
                        whole = wblk[JW * q:JW * q + JW, half * jh:half * jh + half]
                        dst = bass.AP(whole.tensor, whole.offset + 8 * q,
                                      [list(whole.ap[0]), [T * 32, GB], [8 * 32, 2], [33, 8]])
                        pool.tensor_copy(dst, src).then_inc(w_blk, 1)
                        pool.wait_ge(w_blk, g * (2 * Q) + (Q * jh + q + 1))

                def group(g, par, last=False):
                    weights(g, 0)
                    if not last:
                        operand(g + 1)
                        split(g + 1, 1 - par)
                    weights(g, 1)

                operand(0)
                split(0, 0)
                group(0, 0)
                with pool.Fori(0, NG // 2 - 1) as i:
                    group(i * 2 + 1, 1)
                    group(i * 2 + 2, 0)
                group(NG - 1, 1, last=True)

            @block.tensor
            def _(pe):
                def operand(g):
                    pe.wait_ge(x1s_ready, g + 1)
                    if not (isinstance(g, int) and g < 1):
                        pe.wait_ge(xf_ready, g)
                    if not (isinstance(g, int) and g < 3):
                        pe.wait_ge(gsT_ready, g - 2)
                    for a in range(GB):
                        pe.matmul(psX[0:N, D * a:D * a + D], x1s[:, N * a:N * a + N], wt["Wag"][:],
                                  start=(a == 0), stop=True, skip_group_check=True)
                        pe.matmul(psX[N:P, D * a:D * a + D], x1s[:, N * a:N * a + N], wt["Wbg"][:],
                                  start=(a == 0), stop=False, skip_group_check=True)
                    pe.matmul(psX[N:P, :], ones[0:1, 0:N], be1row[0:1, :].unsqueeze(1).broadcast_to([1, GB, D]),
                              start=False, stop=True, skip_group_check=True).then_inc(x_psum, 1)

                def gather(g, c):
                    jh, t0, nt = chunk(c)
                    if c % (CK // JH) == 0:
                        pe.wait_ge(op_in[jh], g * LOADS + LOADS)
                    k = g * CK + c
                    if not (isinstance(k, int) and k < 2):
                        pe.wait_ge(z_ready, k - 1)
                    for j in range(nt):
                        t = t0 + j
                        tb = t // (T // TB)
                        ins = pe.matmul(hbuf[c % 2][:, GB * D * j:GB * D * j + GB * D], pick[jh][0:R_END, P * t:P * t + P],
                                        nodes[jh][0:R_END, GB * D * tb:GB * D * tb + GB * D], start=True, stop=True)
                    ins.then_inc(h_ready, 1)

                def weigh(g, c):
                    jh, t0, nt = chunk(c)
                    pe.wait_ge(g_ready, g * CK + (c + 1))
                    if c % (CK // JH) == 0:
                        pe.wait_ge(w_blk, g * (2 * Q) + Q * (jh + 1))
                    if c == 0:
                        pe.wait_ge(gs_ready, g)
                    for j in range(nt):
                        t = t0 + j
                        hf = t // 8
                        for a in range(GB):
                            blk = ((jh * GB + a) * T + t) * 32
                            ins = pe.matmul(psS[32 * a:32 * a + 32, D * hf:D * hf + D], wblk[:, blk:blk + 32],
                                            z[c % 4][:, GB * D * j + D * a:GB * D * j + D * a + D],
                                            start=(c == 0 and j == 0), stop=(jh == 1 and t % 8 == 7), skip_group_check=True)
                    ins.then_inc(sum_done, 1)

                def turn(g, last=False):
                    pe.wait_ge(gs_ready, g + 1)
                    if not last:
                        pe.wait_ge(xf_ready, g + 3)
                    for hf in range(2):
                        ins = pe.transpose(psT[:, P * hf:P * hf + P], gs[:, D * hf:D * hf + D], ident)
                    ins.then_inc(gsT_psum, 1)

                def group(g, first=False, last=False):
                    for c in range(CK):
                        gather(g, c)
                        if c >= LAG:
                            weigh(g, c - LAG)
                        elif not first:
                            weigh(g - 1, c + CK - LAG)
                        if c == OPERAND and not last:
                            operand(g + 1)
                        if c == TURN and not first:
                            turn(g - 1, last)

                operand(0)
                group(0, first=True)
                with pe.Fori(0, NG // 2 - 1) as i:
                    group(i * 2 + 1)
                    group(i * 2 + 2)
                group(NG - 1, last=True)
                for c in range(CK - LAG, CK):
                    weigh(NG - 1, c)
                pe.wait_ge(gsT_ready, NG - 1)
                turn(NG - 1, last=True)

            @block.vector
            def _(v):
                def group(g, par, half):
                    for c in range(CK):
                        jh, t0, nt = chunk(c)
                        k = g * CK + c
                        v.wait_ge(h_ready, k + 1)
                        if not (isinstance(k, int) and k < 4):
                            v.wait_ge(sum_done, k - 3)
                        r = rE[:, bass.ds(g * GE + GB * T * jh, GB * T)].rearrange("p (g t) -> p t g", t=T)[:, t0:t0 + nt, :]
                        v.tensor_tensor(z[c % 4][:, 0:GB * D * nt].rearrange("p (t g f) -> p t g f", g=GB, f=D),
                                        hbuf[c % 2][:, 0:GB * D * nt].rearrange("p (t g f) -> p t g f", g=GB, f=D),
                                        r.unsqueeze(3).broadcast_to([P, nt, GB, D]), ALU.mult).then_inc(z_ready, 1)
                steps(v, NG, group, 2, 0)

            @block.scalar
            def _(act):
                def sums(g):
                    act.wait_ge(sum_done, g * CK + CK)
                    if not (isinstance(g, int) and g < 1):
                        act.wait_ge(gsT_psum, g)
                    act.copy(gs[:], psS[:, 0:2 * D]).then_inc(gs_ready, 1)

                def keep(g):
                    act.wait_ge(gsT_psum, g + 1)
                    for hf in range(2):
                        dst = gsT[:, bass.ds(g * (GB * N), GB * N)].rearrange("p (g h t q) -> p h g q t", g=GB, h=2, q=Q)[:, hf]
                        ins = act.copy(dst, psT[:, P * hf:P * hf + P].rearrange("p (g q t) -> p g q t", g=GB, q=Q))
                    ins.then_inc(gsT_ready, 1)

                def operand(g, par):
                    act.wait_ge(x_psum, g + 1)
                    if not (isinstance(g, int) and g < 1):
                        act.wait_ge(x_lo, g)
                    if not (isinstance(g, int) and g < 2):
                        act.wait_ge(x_out, g * 16 - 16)
                    act.copy(Xf[:], psX[:])
                    act.copy(Xhi[par], psX[:]).then_inc(xf_ready, 1)

                def group(g, par, first=False, last=False):
                    for c in range(CK):
                        n = GB * D * chunk(c)[2]
                        act.wait_ge(z_ready, g * CK + (c + 1))
                        act.activation(z[c % 4][:, 0:n], z[c % 4][:, 0:n], ACT.Gelu).then_inc(g_ready, 1)
                        if c == LAG - 2 and not first:
                            sums(g - 1)
                        if c == OPERAND + 1 and not last:
                            operand(g + 1, 1 - par)
                        if c == TURN + 1 and not first:
                            keep(g - 1)

                operand(0, 0)
                group(0, 0, first=True)
                with act.Fori(0, NG // 2 - 1) as i:
                    group(i * 2 + 1, 1)
                    group(i * 2 + 2, 0)
                group(NG - 1, 1, last=True)
                sums(NG - 1)
                keep(NG - 1)

        hc = hT
        msg = stage
        adm = [big[:, 512 * i:512 * i + 512] for i in range(2)]
        sq = [big[:, 1024 + 512 * i:1536 + 512 * i] for i in range(2)]
        sd = [big[:, 2048 + 512 * i:2560 + 512 * i] for i in range(2)]
        ad_in = [sem(f"ad_in{i}") for i in range(2)]
        m_psum, m_done, n_psum, n_done, v_psum, sd_done, rr_done, u_done = map(
            sem, ("m_psum", "m_done", "n_psum", "n_done", "v_psum", "sd_done", "rr_done", "u_done"))
        with nc.Block() as block:
            @block.sync
            def _(sp):
                for k in range(NC):
                    if k >= 2:
                        sp.wait_ge(m_psum, k - 1)
                    sp.dma_start(adm[k % 2], adM_d[k]).then_inc(ad_in[k % 2], 16)

            @block.tensor
            def _(pe):
                def message(k):
                    pe.wait_ge(ad_in[k % 2], 16 * (k // 2 + 1))
                    if k >= 1:
                        pe.wait_ge(m_done, k)
                    pe.matmul(bank[0][:], wt["We2"][:], gsT[:, CH * k:CH * k + CH], start=True, stop=False)
                    pe.matmul(bank[0][:], be2_b[:], adm[k % 2], start=False, stop=True).then_inc(m_psum, 1)

                def hidden(k):
                    pe.wait_ge(m_done, k + 1)
                    if k >= 1:
                        pe.wait_ge(n_done, 2 * k)
                    pe.matmul(bank[1][:], wt["Wna"][:], x1T[:, CH * k:CH * k + CH], start=True, stop=False)
                    pe.matmul(bank[1][:], wt["Wnb"][:], msg[k % 2][:], start=False, stop=True).then_inc(n_psum, 1)

                def variance(k):
                    pe.wait_ge(n_done, 2 * k + 2)
                    if k >= 1:
                        pe.wait_ge(sd_done, k)
                    pe.matmul(bank[2][:], ones[:], sq[k % 2], start=True, stop=True).then_inc(v_psum, 1)

                for k in range(NC + 2):
                    if k < NC:
                        message(k)
                    if 1 <= k <= NC:
                        hidden(k - 1)
                    if k >= 2:
                        variance(k - 2)

            @block.scalar
            def _(act):
                for k in range(NC + 2):
                    if k < NC:
                        act.wait_ge(m_psum, k + 1)
                        if k >= 2:
                            act.wait_ge(n_psum, k - 1)
                        act.copy(msg[k % 2][:], bank[0][:]).then_inc(m_done, 1)
                    if 1 <= k <= NC:
                        c = slice(CH * (k - 1), CH * k)
                        act.wait_ge(n_psum, k)
                        if k >= 3:
                            act.wait_ge(v_psum, k - 2)
                        act.activation(hc[:, c], bank[1][:], ACT.Identity, bias=cols[:, BN1C:BN1C + 1]).then_inc(n_done, 1)
                        act.activation(sq[(k - 1) % 2], bank[1][:], ACT.Square, bias=cols[:, BN1C:BN1C + 1]).then_inc(n_done, 1)
                    if k >= 2:
                        act.wait_ge(v_psum, k - 1)
                        if k >= 4:
                            act.wait_ge(u_done, k - 3)
                        act.activation(sd[k % 2], bank[2][:], ACT.Sqrt, scale=1.0 / D, bias=cols[:, EPSC + 1:EPSC + 2]).then_inc(sd_done, 1)

            @block.vector
            def _(v):
                for k in range(NC):
                    c = slice(CH * k, CH * k + CH)
                    v.wait_ge(sd_done, k + 1)
                    v.reciprocal(sd[k % 2], sd[k % 2]).then_inc(rr_done, 1)
                    v.wait_ge(rr_done, k + 1)
                    v.wait_ge(n_done, 2 * k + 2)
                    v.tensor_tensor(hc[:, c], hc[:, c], sd[k % 2], ALU.mult).then_inc(u_done, 1)

        g2 = [big[:, 512 * i:512 * i + 512] for i in range(2)]
        ob = [big[:, 1024 + 512 * i:1536 + 512 * i] for i in range(2)]
        xs = [big[:, 2048 + 512 * i:2560 + 512 * i] for i in range(2)]
        g2_done, o_psum, o_done = map(sem, ("g2_done", "o_psum", "o_done"))
        o_out = [sem(f"o_out{i}") for i in range(2)]
        out_rows = out.rearrange("b n d -> (b n) d")
        with nc.Block() as block:
            @block.scalar
            def _(act):
                for k in range(NC):
                    if k >= 2:
                        act.wait_ge(o_psum, k - 1)
                    act.activation(g2[k % 2], hc[:, CH * k:CH * k + CH], ACT.Gelu, scale=cols[:, GN:GN + 1],
                                   bias=cols[:, BGN:BGN + 1]).then_inc(g2_done, 1)

            @block.tensor
            def _(pe):
                for k in range(NC):
                    pe.wait_ge(g2_done, k + 1)
                    if k >= 2:
                        pe.wait_ge(o_done, k - 1)
                    o = bank[k % 2]
                    for c in range(PAIRS):
                        r = slice(P * c, P * c + P)
                        pe.matmul(o[:, r], g2[k % 2][:, r], wt["Wn2"][:], start=(c == 0), stop=False, skip_group_check=True)
                        pe.matmul(o[:, r], x1T[:, CH * k + P * c:CH * k + P * c + P], ident, start=False, stop=False, skip_group_check=True)
                        ins = pe.matmul(o[:, r], ones[0:1, :], bn2row[0:1, :], start=False, stop=True, skip_group_check=True)
                    ins.then_inc(o_psum, 1)

            @block.vector
            def _(v):
                for k in range(NC):
                    v.wait_ge(o_psum, k + 1)
                    if k >= 2:
                        v.wait_ge(o_out[k % 2], 16 * (k // 2))
                    v.tensor_copy(ob[k % 2], bank[k % 2][:]).then_inc(o_done, 1)

            @block.sync
            def _(sp):
                for k in range(NC):
                    sp.wait_ge(o_done, k + 1)
                    sp.dma_start(out_rows[CH * k:CH * k + CH, :].rearrange("(c p) d -> p c d", p=P),
                                 ob[k % 2].rearrange("p (c d) -> p c d", d=D)).then_inc(o_out[k % 2], 16)
                for p in range(2):
                    sp.wait_ge(o_out[p], 16 * (NC // 2))


NAMES = ["L0_gnn_W", "L0_gnn_b", "L0_gnn_gamma", "L0_gnn_beta", "L1_gnn_We1", "L1_gnn_be1", "L1_gnn_ge", "L1_gnn_bge",
         "L1_gnn_We2", "L1_gnn_be2", "L1_gnn_Wn1", "L1_gnn_bn1", "L1_gnn_gn", "L1_gnn_bgn", "L1_gnn_Wn2", "L1_gnn_bn2"]


def kernel(**inputs):
    import concourse.bacc as bacc
    from concourse.bass_utils import run_bass_kernel_spmd

    nc = bacc.Bacc("TRN2", target_bir_lowering=False, num_devices=1)
    arrays = {f"in_{n}": np.ascontiguousarray(inputs[n]) for n in ["x", "adj"] + NAMES}
    arrays["in_consts"] = constants()
    ap = {n: nc.dram_tensor(n, a.shape, mybir.dt.from_np(a.dtype), kind="ExternalInput").ap() for n, a in arrays.items()}
    out = nc.dram_tensor("out", (NB, N, D), F32, kind="ExternalOutput").ap()
    build(nc, ap["in_x"], ap["in_adj"], ap["in_consts"], {n: ap[f"in_{n}"] for n in NAMES}, out)
    r = run_bass_kernel_spmd(nc, [arrays], core_ids=[0])
    return r.results[0]["out"]
```

```python
from contextlib import ExitStack

import numpy as np

import concourse.bass as bass
from concourse import mybir

F32 = mybir.dt.float32
F32R = mybir.dt.float32r
ACT = mybir.ActivationFunctionType
ALU = mybir.AluOpType
AX = mybir.AxisListType

P = 128
NB = 128
N = 64
D = 128
GB = 4
NG = NB // GB
JH = 2
JW = N // JH
Q = P // JW
T = N // Q
GE = JH * GB * T
CH = 512
NC = NB * N // CH
PAIRS = CH // P
EPS0, EPS1 = 1e-3, 1e-5

C_ID, C_OFF, C_OFFE, C_CEN, C_JJ, C_BM, C_ROW, C_SEL = 0, 128, 256, 384, 512, 544, 552, 554
C_ALL = C_SEL + T * P

TB = 4
AW = N // TB
R_B, R_A, R_S, R_C = 0, 2 * JW, 2 * JW + 2 * AW, 2 * JW + 2 * AW + 4 * GB
R_END = R_C + 2
CT = 2
CW = CT * GB * D
CK = JH * T // CT
LAG = 4
RING = 8
OPERAND = {c: (c,) for c in range(GB)}
TURN = 7


def constants():
    c = np.zeros((P, C_ALL), np.float32)
    eye = np.eye(P, dtype=np.float32)
    c[:, C_ID:C_ID + P] = eye
    c[:, C_OFF:C_OFF + P] = 1 - eye
    c[:, C_CEN:C_CEN + P] = eye - 1.0 / D
    e = np.arange(P)
    q, jj = e // JW, e % JW
    for jh in range(JH):
        for g in range(GB):
            for t in range(T):
                c[:, C_OFFE + (jh * GB + g) * T + t] = Q * t + q != JW * jh + jj
    c[e, C_JJ + jj] = 1
    for part in range(4):
        for g in range(GB):
            c[R_S + GB * part + g, C_BM + 4 * (part % 2) + g] = 1
    for part in range(2):
        c[R_C + part, C_BM + 4 * part:C_BM + 4 * part + GB] = 1
    c[:R_C, C_ROW], c[R_C:, C_ROW + 1] = 1, 1
    sel = c[:, C_SEL:].reshape(P, T, P)
    sel[R_C:R_END] = 1
    for t in range(T):
        for lo in (0, 1):
            sel[R_B + 2 * jj + lo, t, e] = 1
            sel[R_A + 2 * (Q * (t % (T // TB)) + q) + lo, t, e] = 1
    return c


def steps(eng, n, body, head, tail):
    assert head % 2 == 0 and (n - head - tail) % 2 == 0
    for k in range(head):
        body(k, k % 2, k // 2)
    with eng.Fori(0, (n - head - tail) // 2) as i:
        body(i * 2 + head, 0, i + head // 2)
        body(i * 2 + head + 1, 1, i + head // 2)
    for k in range(n - tail, n):
        body(k, k % 2, k // 2)


def build(nc, x, adj, consts, w, out):
    with ExitStack() as ctx:
        def sb(name, shape, dt=F32):
            return ctx.enter_context(nc.sbuf_tensor(name, shape, dt))

        def sem(name):
            return ctx.enter_context(nc.semaphore(name))

        psum = ctx.enter_context(nc.psum_tensor("psum", [P, 8 * 512], F32))
        bank = [psum[:, 512 * i:512 * i + 512] for i in range(8)]

        x1T = sb("x1T", [P, NB * N])
        hT = sb("hT", [P, NB * N])
        wE = sb("wE", [P, NG * GE])
        rE = sb("rE", [P, NG * GE])
        cst = sb("cst", [P, C_SEL])
        wt = {n: sb(n, [P, D]) for n in ("W", "Wa", "Wb", "Wmsg", "Wna", "Wnb", "Wn2", "Wag", "Wbg")}
        ge_b = sb("ge_b", [P, D])
        bge_b = sb("bge_b", [P, D])
        vmsg = sb("vmsg", [P, D])
        cols = sb("cols", [P, 16])
        B0, GAM, BET, BE1, BN1, GN, BGN, BE1C, BN1C, EPSC, BN2, MEAN4 = 0, 1, 2, 3, 4, 5, 6, 7, 8, 9, 11, 12
        ones = sb("ones", [P, D])
        bn1_b = sb("bn1_b", [P, D])
        ident = cst[:, C_ID:C_ID + P]
        pick = [sb(f"pick{i}", [P, T * P], F32R) for i in range(JH)]
        nodes = [sb(f"nodes{i}", [P, TB * GB * D], F32R) for i in range(JH)]
        big = sb("big", [P, RING * CW])
        wblk = sb("wblk", [P, JH * GB * T * 32])
        Xf = sb("Xf", [P, GB * D])
        X2 = [sb(f"X2_{i}", [P, 2 * GB * D], F32R) for i in range(2)]
        Xhi = [x2[:, 0:GB * D] for x2 in X2]
        Xlo = [x2[:, GB * D:2 * GB * D] for x2 in X2]
        x1s = sb("x1s", [P, GB * N])
        gs = sb("gs", [P, 2 * D])

        adM_d = nc.dram_tensor("adM_d", [NC, P, CH], F32, kind="Internal").ap()
        s_d = nc.dram_tensor("s_d", [NG, JH, 2, GB * T, P], F32, kind="Internal").ap()
        x_d = nc.dram_tensor("x_d", [NG, 2 * P, GB * D], F32, kind="Internal").ap()

        w_in, c_in, w_ready, w_psum, w_cols, w_row = map(sem, ("w_in", "c_in", "w_ready", "w_psum", "w_cols", "w_row"))
        col_of = {"L0_gnn_b": B0, "L0_gnn_gamma": GAM, "L0_gnn_beta": BET, "L1_gnn_be1": BE1,
                  "L1_gnn_bn1": BN1, "L1_gnn_gn": GN, "L1_gnn_bgn": BGN, "L1_gnn_bn2": BN2}
        turned = big[:, 2048:2048 + 2 * D]
        with nc.Block() as block:
            @block.sync
            def _(sp):
                n = 0
                for dst, src in ([(cst[:], consts[:, 0:C_SEL]), (big[:, 0:T * P], consts[:, C_SEL:C_ALL]),
                                  (wt["W"][:], w["L0_gnn_W"]), (wt["Wa"][:], w["L1_gnn_We1"][0:D, :]),
                                  (wt["Wb"][:], w["L1_gnn_We1"][D:2 * D, :]), (wt["Wmsg"][:], w["L1_gnn_We2"]),
                                  (wt["Wna"][:], w["L1_gnn_Wn1"][0:D, :]), (wt["Wnb"][:], w["L1_gnn_Wn1"][D:2 * D, :]),
                                  (wt["Wn2"][:], w["L1_gnn_Wn2"]),
                                  (ge_b[:], w["L1_gnn_ge"].partition_broadcast(P)),
                                  (bge_b[:], w["L1_gnn_bge"].partition_broadcast(P)),
                                  (vmsg[:], w["L1_gnn_be2"].partition_broadcast(P))]):
                    sp.dma_start(dst, src).then_inc(w_in, 16)
                    n += 16
                assert n == 16 * 12

            @block.gpsimd
            def _(pool):
                for name, c in col_of.items():
                    pool.dma_start(cols[:, c:c + 1], w[name].unsqueeze(1)).then_inc(c_in, 16)

            @block.tensor
            def _(pe):
                pe.wait_ge(w_in, 192)
                pe.wait_ge(c_in, 128)
                pe.matmul(bank[0][:, 0:2], cst[:, C_CEN:C_CEN + P], cols[:, BE1:BE1 + 2], start=True, stop=True).then_inc(w_psum, 1)
                pe.wait_ge(w_cols, 1)
                pe.matmul(bank[1][:, 0:D], cols[:, BE1C:BE1C + 1].broadcast_to([P, P]), ident, start=True, stop=True).then_inc(w_psum, 1)
                pe.matmul(bank[4][:, 0:D], cols[:, BN1C:BN1C + 1].broadcast_to([P, P]), ident, start=True, stop=True)
                pe.transpose(bank[2][:, 0:D], wt["Wmsg"][:], ident)
                pe.transpose(bank[2][:, D:2 * D], vmsg[:], ident).then_inc(w_psum, 1)
                pe.wait_ge(w_cols, 2)
                pe.matmul(bank[3][:, 0:D], turned[:, 0:D], wt["Wnb"][:], start=True, stop=True, skip_group_check=True)
                pe.matmul(bank[3][:, D:2 * D], turned[:, D:2 * D], wt["Wnb"][:], start=False, stop=True,
                          skip_group_check=True).then_inc(w_psum, 1)

            @block.scalar
            def _(act):
                act.wait_ge(w_in, 192)
                for jh in range(JH):
                    act.copy(pick[jh][0:R_END, :], big[0:R_END, 0:T * P])
                act.wait_ge(w_row, 6 + 2 * GB)
                act.copy(nodes[1][R_S:R_END, :].rearrange("p (b n) -> p b n", b=TB),
                         big[R_S:R_END, 5400:5400 + GB * D].unsqueeze(1).broadcast_to([R_END - R_S, TB, GB * D]))

            @block.vector
            def _(v):
                v.memset(ones[:], 1.0)
                v.memset(wblk[:], 0.0)
                v.memset(cols[:, EPSC:EPSC + 1], EPS0)
                v.memset(cols[:, EPSC + 1:EPSC + 2], EPS1).then_inc(w_ready, 1)
                v.wait_ge(w_in, 192)
                r = 1
                for i, name in enumerate(("Wa", "Wb", "Wna", "Wnb")):
                    m = cols[:, MEAN4 + i:MEAN4 + i + 1]
                    v.tensor_reduce(m, wt[name][:], AX.X, ALU.add).then_inc(w_ready, 1)
                    v.wait_ge(w_ready, r + 1)
                    v.tensor_scalar(m, m, 1.0 / D, None, ALU.mult).then_inc(w_ready, 1)
                    v.wait_ge(w_ready, r + 2)
                    v.tensor_scalar(wt[name][:], wt[name][:], m, None, ALU.subtract).then_inc(w_ready, 1)
                    r += 3
                v.wait_ge(w_ready, r)
                v.tensor_tensor(wt["Wag"][:], wt["Wa"][:], ge_b[:], ALU.mult)
                v.tensor_tensor(wt["Wbg"][:], wt["Wb"][:], ge_b[:], ALU.mult)
                v.wait_ge(w_psum, 1)
                v.tensor_copy(cols[:, BE1C:BE1C + 2], bank[0][:, 0:2]).then_inc(w_cols, 1)
                v.wait_ge(w_psum, 2)
                v.wait_ge(w_psum, 3)
                v.tensor_copy(turned, bank[2][:, 0:2 * D]).then_inc(w_cols, 1)
                rows = slice(R_S, R_END)
                be1_g, row_b = big[rows, 4800:4800 + D], big[rows, 4600:4600 + D]
                v.tensor_tensor(be1_g, bank[1][rows, 0:D], ge_b[rows, :], ALU.mult).then_inc(w_row, 1)
                v.wait_ge(w_psum, 4)
                v.tensor_copy(bn1_b[:], bank[4][:, 0:D])
                v.tensor_copy(wt["Wmsg"][:], bank[3][:, 0:D])
                v.tensor_copy(vmsg[:], bank[3][:, D:2 * D])
                v.wait_ge(w_row, 1)
                v.tensor_scalar(be1_g, be1_g, cst[rows, C_ROW + 1:C_ROW + 2], None, ALU.mult).then_inc(w_row, 1)
                v.wait_ge(w_row, 2)
                v.scalar_tensor_tensor(out=row_b, in0=bge_b[rows, :], scalar=cst[rows, C_ROW:C_ROW + 1], in1=be1_g,
                                       op0=ALU.mult, op1=ALU.add).then_inc(w_row, 1)
                v.wait_ge(w_row, 3)
                hi, lo, hi_g = big[rows, 5000:5000 + D], big[rows, 5200:5200 + D], big[rows, 5400:5400 + GB * D]
                v.tensor_copy(nodes[0][rows, 0:D], row_b).then_inc(w_row, 1)
                v.wait_ge(w_row, 4)
                v.tensor_copy(hi, nodes[0][rows, 0:D].bitcast(F32)).then_inc(w_row, 1)
                v.wait_ge(w_row, 5)
                v.tensor_tensor(lo, row_b, hi, ALU.subtract).then_inc(w_row, 1)
                for g in range(GB):
                    v.tensor_scalar(hi_g[:, D * g:D * g + D], hi, cst[rows, C_BM + g:C_BM + g + 1], None, ALU.mult).then_inc(w_row, 1)
                v.wait_ge(w_row, 6 + GB)
                for g in range(GB):
                    v.scalar_tensor_tensor(out=hi_g[:, D * g:D * g + D], in0=lo, scalar=cst[rows, C_BM + 4 + g:C_BM + 5 + g],
                                           in1=hi_g[:, D * g:D * g + D], op0=ALU.mult, op1=ALU.add).then_inc(w_row, 1)
                v.wait_ge(w_row, 6 + 2 * GB)
                v.tensor_copy(nodes[0][rows, :].rearrange("p (b n) -> p b n", b=TB),
                              hi_g.unsqueeze(1).broadcast_to([R_END - R_S, TB, GB * D]))

        xin = [hT[:, CH * k:CH * k + CH] for k in range(NC)]
        adin = [big[:, 512 * i:512 + 512 * i] for i in range(4)]
        lin = [rE[:, 256 * k:256 + 256 * k] for k in range(NC)]
        adT = [big[:, 2560 + 512 * i:3072 + 512 * i] for i in range(2)]
        adM = [big[:, 3584 + 512 * i:4096 + 512 * i] for i in range(2)]
        yT = [big[:, 4608 + 512 * i:5120 + 512 * i] for i in range(2)]
        bn = wblk[:, 0:NB * 6]
        sc = Xf
        in0 = [sem(f"in0_{i}") for i in range(2)]
        z0, t_done, xT_done, adT_done, y_done, yT_done, h_done, hT_done, bn_done = map(
            sem, ("z0", "t_done", "xT_done", "adT_done", "y_done", "yT_done", "h_done", "hT_done", "bn_done"))
        adM_out = [sem(f"adM_out{i}") for i in range(2)]
        x_rows = x.rearrange("b n d -> (b n) d")
        t_banks = [(bank[0], bank[1], bank[2]), (bank[5], bank[6], bank[7])]
        with nc.Block() as block:
            @block.sync
            def _(sp):
                sp.wait_ge(z0, 1)
                for k2 in range(NC // 2):
                    p = k2 % 2
                    if k2 >= 2:
                        sp.wait_ge(t_done, 2 * k2 - 2)
                    sp.dma_start(hT[:, 2 * CH * k2:2 * CH * k2 + 2 * CH].rearrange("p (c d) -> p c d", d=D),
                                 x_rows[2 * CH * k2:2 * CH * k2 + 2 * CH, :].rearrange("(c p) d -> p c d", p=P)).then_inc(in0[p], 16)
                    for b2 in range(2):
                        sp.dma_start(big[N * b2:N * b2 + N, 2 * CH * p:2 * CH * p + 2 * CH]
                                     .rearrange("p (c b j) -> p c b j", b=2, j=N)[:, :, b2, :],
                                     adj[16 * k2:16 * k2 + 16].rearrange("(c b) i j -> b i c j", b=2)[b2]).then_inc(in0[p], 16)
                    for k in (2 * k2, 2 * k2 + 1):
                        for jh in range(JH):
                            sp.dma_start(lin[k][:, P * jh:P * jh + P].rearrange("p (q j) -> p q j", q=Q),
                                         adj[8 * k:8 * k + 8].rearrange("g (t q) (h j) -> h (g t) q j", q=Q, h=JH)[jh]).then_inc(in0[p], 16)

            @block.tensor
            def _(pe):
                def turn(k):
                    p = k % 4
                    x_bank, ad_bank, lin_bank = t_banks[k % 2]
                    pe.wait_ge(in0[k // 2 % 2], 112 * (k // 4 + 1))
                    if k >= 2:
                        pe.wait_ge(xT_done, k - 1)
                        pe.wait_ge(adT_done, k - 1)
                    for c in range(4):
                        pe.transpose(x_bank[:, 128 * c:128 * c + 128], xin[k][:, 128 * c:128 * c + 128], ident)
                        pe.transpose(ad_bank[:, 128 * c:128 * c + 128], adin[p][:, 128 * c:128 * c + 128], ident)
                    for jh in range(JH):
                        last = pe.transpose(lin_bank[:, P * jh:P * jh + P], lin[k][:, P * jh:P * jh + P], ident)
                    last.then_inc(t_done, 1)

                def neighbours(k):
                    p = k % 2
                    pe.wait_ge(adT_done, k + 1)
                    if k >= 1:
                        pe.wait_ge(yT_done, k)
                    for c in range(4):
                        last = pe.matmul(bank[3][:, 128 * c:128 * c + 128], xin[k][:, 128 * c:128 * c + 128],
                                         adT[p][:, 128 * c:128 * c + 128], start=True, stop=True)
                    last.then_inc(y_done, 1)

                def product(k):
                    pe.wait_ge(yT_done, k + 1)
                    if k >= 1:
                        pe.wait_ge(hT_done, k)
                    pe.matmul(bank[4][:], wt["W"][:], yT[k % 2], start=True, stop=True).then_inc(h_done, 1)

                for k in range(NC + 2):
                    if k < NC:
                        turn(k)
                    if 1 <= k <= NC:
                        neighbours(k - 1)
                    if k >= 2:
                        product(k - 2)

            @block.scalar
            def _(act):
                for k in range(NC + 2):
                    if k < NC:
                        act.wait_ge(t_done, k + 1)
                        act.copy(x1T[:, CH * k:CH * k + CH], t_banks[k % 2][0][:]).then_inc(xT_done, 1)
                    if 1 <= k <= NC:
                        act.wait_ge(adT_done, k)
                        act.dma_start(adM_d[k - 1], adM[(k - 1) % 2]).then_inc(adM_out[(k - 1) % 2], 16)
                        act.wait_ge(y_done, k)
                        if k >= 3:
                            act.wait_ge(h_done, k - 2)
                        act.copy(yT[(k - 1) % 2], bank[3][:]).then_inc(yT_done, 1)
                    if k >= 2:
                        act.wait_ge(h_done, k - 1)
                        act.activation(hT[:, CH * (k - 2):CH * (k - 1)], bank[4][:], ACT.Identity,
                                       bias=cols[:, B0:B0 + 1]).then_inc(hT_done, 1)
                for p in range(2):
                    act.wait_ge(adM_out[p], 16 * (NC // 2))

            @block.vector
            def _(v):
                for k in range(NC + 2):
                    p = k % 2
                    if k < NC:
                        v.wait_ge(t_done, k + 1)
                        if k >= 2:
                            v.wait_ge(y_done, k - 1)
                            v.wait_ge(adM_out[p], 16 * (k // 2))
                        _, ad_bank, lin_bank = t_banks[p]
                        v.tensor_copy(adT[p], ad_bank[:])
                        v.tensor_tensor(adM[p].rearrange("p (c n) -> p c n", n=P), ad_bank[:].rearrange("p (c n) -> p c n", n=P),
                                        cst[:, C_OFF:C_OFF + P].unsqueeze(1).broadcast_to([P, PAIRS, P]), ALU.mult)
                        v.tensor_tensor(wE[:, 256 * k:256 * k + 256].rearrange("p (c h r) -> p c h r", c=2, h=JH),
                                        lin_bank[:, 0:256].rearrange("p (h c r) -> p c h r", c=2, h=JH),
                                        cst[:, C_OFFE:C_OFFE + P].rearrange("p (h r) -> p h r", h=JH)
                                        .unsqueeze(1).broadcast_to([P, 2, JH, GB * T]), ALU.mult).then_inc(adT_done, 1)
                    if k >= 2:
                        v.wait_ge(hT_done, k - 1)
                        for b in range(8 * (k - 2), 8 * (k - 1)):
                            last = v.bn_stats(bn[:, 6 * b:6 * b + 6], hT[:, N * b:N * b + N])
                        last.then_inc(bn_done, 1)

            @block.gpsimd
            def _(pool):
                pool.memset(big[:, 0:4 * CH], 0.0).then_inc(z0, 1)

        a_dve, a_var, a_sd = map(sem, ("a_dve", "a_var", "a_sd"))
        with nc.Block() as block:
            @block.vector
            def _(v):
                n = 0

                def then(ins):
                    nonlocal n
                    n += 1
                    ins.then_inc(a_dve, 1)
                    v.wait_ge(a_dve, n)
                st = bn.rearrange("p (b s) -> p b s", s=6)
                me, ve, mo, vo = (st[:, :, i] for i in (1, 2, 4, 5))
                mean, var, tmp = big[:, 0:128], big[:, 128:256], big[:, 256:384]
                scale, shift = sc[:, 0:128], sc[:, 128:256]
                then(v.tensor_tensor(mean, me, mo, ALU.add))
                then(v.tensor_tensor(tmp, me, mo, ALU.subtract))
                then(v.tensor_tensor(tmp, tmp, tmp, ALU.mult))
                then(v.tensor_tensor(var, ve, vo, ALU.add))
                then(v.tensor_scalar(var, var, 1.0 / N, None, ALU.mult))
                then(v.tensor_scalar(mean, mean, 0.5, None, ALU.mult))
                v.scalar_tensor_tensor(out=var, in0=tmp, scalar=0.25, in1=var, op0=ALU.mult, op1=ALU.add).then_inc(a_var, 1)
                v.wait_ge(a_sd, 1)
                then(v.reciprocal(scale, tmp))
                then(v.tensor_scalar(scale, scale, cols[:, GAM:GAM + 1], None, ALU.mult))
                then(v.tensor_tensor(tmp, mean, scale, ALU.mult))
                v.tensor_scalar(shift, tmp, -1.0, cols[:, BET:BET + 1], ALU.mult, ALU.add)

            @block.scalar
            def _(act):
                act.wait_ge(a_var, 1)
                act.activation(big[:, 256:384], big[:, 128:256], ACT.Sqrt, bias=cols[:, EPSC:EPSC + 1]).then_inc(a_sd, 1)

        AT = [big[:, 0 + 512 * i:512 + 512 * i] for i in range(2)]
        BT = [big[:, 1024 + 512 * i:1536 + 512 * i] for i in range(2)]
        A2 = [big[:, 2048 + 512 * i:2560 + 512 * i] for i in range(2)]
        B2 = [big[:, 3072 + 512 * i:3584 + 512 * i] for i in range(2)]
        own = big[:, 4608:4608 + CH]
        b2s = [big[:, 4112 + 16 * i:4128 + 16 * i] for i in range(2)]
        sE = hT[:, 0:NG * GE]
        ab_psum, ab_done, bb_psum, jj_done, bb_done, gram_done, add_done, var_done, sq_done, st_psum, st_hi, st_done = map(
            sem, ("ab_psum", "ab_done", "bb_psum", "jj_done", "bb_done", "gram_done", "add_done", "var_done", "sq_done",
                  "st_psum", "st_hi", "st_done"))
        s_out = [sem(f"s_out{i}") for i in range(2)]
        hm_done, hn_done, silu_done, x1_done = map(sem, ("hm_done", "hn_done", "silu_done", "x1_done"))

        def store_s(sp, k):
            sp.wait_ge(st_done, 2 * k + 2)
            for part, src in enumerate((Xhi[k % 2], Xlo[k % 2])):
                for jh in range(JH):
                    sp.dma_start(s_d[4 * k:4 * k + 4, jh, part].rearrange("c r e -> r c e"),
                                 src[GB * T * jh:GB * T * (jh + 1), :].bitcast(F32).rearrange("p (c e) -> p c e", e=P)
                                 ).then_inc(s_out[k % 2], 16)

        psX = bank[6]
        x1s_ready, x_psum, xf_ready, x_lo, x_out = map(sem, ("x1s_ready", "x_psum", "xf_ready", "x_lo", "x_out"))

        def copy_x(pool, g):
            if not (isinstance(g, int) and g < 1):
                pool.wait_ge(x_psum, g)
            pool.tensor_copy(x1s[:], x1T[:, bass.ds(g * (GB * N), GB * N)]).then_inc(x1s_ready, 1)
            pool.wait_ge(x1s_ready, g + 1)

        def split_x(pool, g, par):
            pool.wait_ge(xf_ready, g + 1)
            pool.tensor_tensor(Xlo[par], Xf[:], Xhi[par].bitcast(F32), ALU.subtract).then_inc(x_lo, 1)
            pool.wait_ge(x_lo, g + 1)

        def operand(pe, g, a):
            if a == 0:
                pe.wait_ge(x1s_ready, g + 1)
                if not (isinstance(g, int) and g < 1):
                    pe.wait_ge(xf_ready, g)
            pe.matmul(psX[0:N, D * a:D * a + D], x1s[:, N * a:N * a + N], wt["Wag"][:],
                      start=(a == 0), stop=True, skip_group_check=True)
            ins = pe.matmul(psX[N:P, D * a:D * a + D], x1s[:, N * a:N * a + N], wt["Wbg"][:],
                            start=(a == 0), stop=True, skip_group_check=True)
            if a == GB - 1:
                ins.then_inc(x_psum, 1)

        def keep_x(act, g, par):
            act.wait_ge(x_psum, g + 1)
            if not (isinstance(g, int) and g < 1):
                act.wait_ge(x_lo, g)
            if isinstance(g, int) and g < 2:
                act.wait_ge(s_out[par], 64 * (NC // 4))
            else:
                act.wait_ge(x_out, g * 16 - 16)
            act.copy(Xf[:], psX[:])
            act.copy(Xhi[par], psX[:]).then_inc(xf_ready, 1)

        def store_x(sp, g, par):
            sp.wait_ge(x_lo, g + 1)
            sp.dma_start(x_d[bass.ds(g, 1)].rearrange("o (p h) n -> (o p) h n", h=2),
                         X2[par][:].bitcast(F32).rearrange("p (h n) -> p h n", h=2)).then_inc(x_out, 16)

        half = lambda k: slice(256 * (k % 2), 256 * (k % 2) + 256)
        with nc.Block() as block:
            @block.gpsimd
            def _(pool):
                pool.memset(wblk[:], 0.0)
                pool.wait_ge(x1_done, 1)
                copy_x(pool, 0)
                split_x(pool, 0, 0)

            @block.tensor
            def _(pe):
                def ab(k):
                    pe.wait_ge(x1_done, k + 1)
                    if k >= 2:
                        pe.wait_ge(ab_done, 4 * k - 4)
                    a_bank, b_bank = bank[4 * (k % 2)], bank[4 * (k % 2) + 1]
                    pe.matmul(a_bank[:], wt["Wa"][:], x1T[:, CH * k:CH * k + CH], start=True, stop=True)
                    pe.matmul(b_bank[:], wt["Wb"][:], x1T[:, CH * k:CH * k + CH], start=True, stop=True).then_inc(ab_psum, 1)

                def gram(k):
                    p = k % 2
                    pe.wait_ge(ab_done, 4 * k + 4)
                    if k >= 1:
                        pe.wait_ge(jj_done, k)
                    for gg in range(2):
                        last = pe.matmul(bank[6][:, 256 * gg:256 * gg + 256], ones[:],
                                         B2[p][:, 256 * gg:256 * gg + 256].rearrange("p (g h j) -> p h g j", g=GB, h=JH),
                                         start=(gg == 0), stop=True, skip_group_check=True)
                    last.then_inc(bb_psum, 1)
                    if k >= 2:
                        pe.wait_ge(var_done, k - 1)
                    for gg in range(2):
                        o = bank[2 + p][:, 128 * gg:128 * gg + 128]
                        view = lambda m: m[:, 256 * gg:256 * gg + 256].rearrange("p (g t q) -> p q g t", g=GB, q=Q)
                        for q in range(Q):
                            pe.matmul(o[JW * q:JW * q + JW, :], ones[:, 0:JW],
                                      view(A2[p])[:, q].unsqueeze(1).broadcast_to([P, JH, GB, T]),
                                      start=(gg == 0), stop=False, skip_group_check=True)
                        for jh in range(JH):
                            for g in range(GB):
                                for q in range(Q):
                                    c0 = (jh * GB + g) * T
                                    b0 = 256 * gg + N * g + JW * jh
                                    last = pe.matmul(o[JW * q:JW * q + JW, c0:c0 + T], BT[p][:, b0:b0 + JW],
                                              view(AT[p])[:, q, g], start=False, stop=True, skip_group_check=True)
                    last.then_inc(gram_done, 1)

                def turn(k):
                    pe.wait_ge(sq_done, k + 1)
                    if k >= 1:
                        pe.wait_ge(st_done, k)
                    for c in range(2):
                        last = pe.transpose(bank[7][:, 256 * (k % 2) + P * c:256 * (k % 2) + P * c + P],
                                            sE[:, 256 * k + P * c:256 * k + P * c + P], ident)
                    last.then_inc(st_psum, 1)

                for k in range(NC + 3):
                    if k < NC:
                        ab(k)
                    if 1 <= k <= NC:
                        gram(k - 1)
                    if k == NC:
                        pe.wait_ge(jj_done, NC)
                        for a in range(GB):
                            operand(pe, 0, a)
                    if k >= 3:
                        turn(k - 3)

            @block.scalar
            def _(act):
                def silu(k):
                    h = hT[:, CH * k:CH * k + CH]
                    act.wait_ge(hn_done, k + 1)
                    act.activation(h, h, ACT.Silu).then_inc(silu_done, 1)

                silu(0)
                silu(1)
                for k in range(NC + 4):
                    if k < NC:
                        p = k % 2
                        a_bank, b_bank = bank[4 * p], bank[4 * p + 1]
                        act.wait_ge(ab_psum, k + 1)
                        if k >= 2:
                            act.wait_ge(gram_done, k - 1)
                        act.mul(AT[p], a_bank[:], 2.0).then_inc(ab_done, 1)
                        act.activation(A2[p], a_bank[:], ACT.Square).then_inc(ab_done, 1)
                        act.activation(BT[p], b_bank[:], ACT.Identity, bias=cols[:, BE1C:BE1C + 1]).then_inc(ab_done, 1)
                        act.activation(B2[p], b_bank[:], ACT.Square, bias=cols[:, BE1C:BE1C + 1]).then_inc(ab_done, 1)
                    if k >= 4:
                        batch = (k - 4) // 2
                        act.wait_ge(st_psum, k - 3)
                        if batch >= 2:
                            act.wait_ge(s_out[batch % 2], 64 * (batch // 2))
                        act.copy(Xhi[batch % 2][:, half(k - 4)], bank[7][:, half(k - 4)]).then_inc(st_hi, 1)
                    if 2 <= k <= NC + 1:
                        act.wait_ge(var_done, k - 1)
                        act.activation(sE[:, 256 * (k - 2):256 * (k - 1)], rE[:, 256 * (k - 2):256 * (k - 1)], ACT.Sqrt,
                                       bias=cols[:, EPSC + 1:EPSC + 2]).then_inc(sq_done, 1)
                    if k + 2 < NC:
                        silu(k + 2)
                keep_x(act, 0, 0)

            @block.vector
            def _(v):
                def normalise(k):
                    h = hT[:, CH * k:CH * k + CH].rearrange("p (b n) -> p b n", n=N)
                    nb = CH // N
                    scale, shift = (sc[:, 128 * i + nb * k:128 * i + nb * k + nb].unsqueeze(2).broadcast_to([P, nb, N]) for i in range(2))
                    v.tensor_tensor(h, h, scale, ALU.mult).then_inc(hm_done, 1)
                    v.wait_ge(hm_done, k + 1)
                    v.tensor_tensor(h, h, shift, ALU.add).then_inc(hn_done, 1)

                def add_x(k):
                    c = slice(CH * k, CH * k + CH)
                    v.wait_ge(silu_done, k + 1)
                    v.tensor_tensor(x1T[:, c], x1T[:, c], hT[:, c], ALU.add).then_inc(x1_done, 1)

                normalise(0)
                normalise(1)
                add_x(0)
                normalise(2)
                add_x(1)
                for k in range(NC + 3):
                    if k < NC:
                        c = slice(256 * k, 256 * k + 256)
                        v.wait_ge(bb_psum, k + 1)
                        v.tensor_tensor(own.rearrange("p (c j) -> p c j", j=JW), bank[6][:].rearrange("p (c j) -> p c j", j=JW),
                                        cst[:, C_JJ:C_JJ + JW].unsqueeze(1).broadcast_to([P, CH // JW, JW]), ALU.mult).then_inc(jj_done, 1)
                        v.wait_ge(jj_done, k + 1)
                        v.tensor_reduce(b2s[k % 2], own.rearrange("p (c j) -> p c j", j=JW), AX.X, ALU.add).then_inc(bb_done, 1)
                    if k >= 3:
                        batch = (k - 3) // 2
                        v.wait_ge(st_hi, k - 2)
                        v.tensor_tensor(Xlo[batch % 2][:, half(k - 3)], bank[7][:, half(k - 3)],
                                        Xhi[batch % 2][:, half(k - 3)].bitcast(F32), ALU.subtract).then_inc(st_done, 1)
                    if k + 2 < NC:
                        add_x(k + 2)
                    if k + 3 < NC:
                        normalise(k + 3)
                    if k < NC:
                        v.wait_ge(gram_done, k + 1)
                        v.wait_ge(bb_done, k + 1)
                        v.tensor_tensor(rE[:, c].rearrange("p (c t) -> p c t", t=T),
                                        bank[2 + k % 2][:, 0:256].rearrange("p (c t) -> p c t", t=T),
                                        b2s[k % 2].unsqueeze(2).broadcast_to([P, 2 * JH * GB, T]), ALU.add).then_inc(add_done, 1)
                        v.wait_ge(add_done, k + 1)
                        v.tensor_scalar(rE[:, c], rE[:, c], 1.0 / D, 0.0, ALU.mult, ALU.max).then_inc(var_done, 1)
                    if 1 <= k <= NC:
                        v.wait_ge(sq_done, k)
                        v.reciprocal(rE[:, 256 * (k - 1):256 * k], sE[:, 256 * (k - 1):256 * k])

            @block.sync
            def _(sp):
                for k in range(NC // 2 - 1):
                    store_s(sp, k)
                store_x(sp, 0, 0)

        gsT = hT
        z = [big[:, CW * i:CW * i + CW] for i in range(RING)]
        hbuf = [psum[:, CW * i:CW * i + CW] for i in range(2)]
        psS, psT = bank[4:6], bank[7]
        op_in = [sem(f"op_in{i}") for i in range(JH)]
        w_blk, h_ready, z_ready, g_ready, sum_done, gs_ready, gsT_psum, gsT_ready = map(
            sem, ("w_blk", "h_ready", "z_ready", "g_ready", "sum_done", "gs_ready", "gsT_psum", "gsT_ready"))

        def chunk(c):
            return c // (CK // JH), CT * (c % (CK // JH))

        with nc.Block() as block:
            @block.sync
            def _(sp):
                def load(g, par):
                    if not (isinstance(g, int) and g < 1):
                        store_x(sp, g, par)
                    for jh in range(JH):
                        if not (isinstance(g, int) and g < 1):
                            sp.wait_ge(h_ready, g * CK + (CK // JH * (jh + 1) - CK))
                        elif jh == 0:
                            sp.wait_ge(s_out[0], 64)
                        for part in range(2):
                            r0 = R_S + 2 * GB * part
                            sp.dma_start(pick[jh][r0:r0 + 2 * GB, :].bitcast(F32),
                                         s_d[bass.ds(g, 1), jh, part].rearrange("o (g t) e -> o g (t e)", g=GB)
                                         .broadcast_to([2, GB, T * P])).then_inc(op_in[jh], 16)
                        if jh == 0:
                            sp.wait_ge(x_out, g * 16 + 16)
                        sp.dma_start(nodes[jh][R_A:R_S, :].bitcast(F32).rearrange("p (b n) -> p b n", b=TB),
                                     x_d[bass.ds(g, 1), 0:P].rearrange("o (b p) n -> (o p) b n", b=TB)).then_inc(op_in[jh], 16)
                        b0 = P + 2 * JW * jh
                        sp.dma_start(nodes[jh][R_B:R_A, :].bitcast(F32).rearrange("p (b n) -> p b n", b=TB),
                                     x_d[bass.ds(g, 1), b0:b0 + 2 * JW].rearrange("o p n -> (o p) n")
                                     .unsqueeze(1).broadcast_to([2 * JW, TB, GB * D])).then_inc(op_in[jh], 16)
                load(0, 0)
                store_s(sp, NC // 2 - 1)
                load(1, 1)
                for p in range(2):
                    sp.wait_ge(s_out[p], 64 * (NC // 4))
                with sp.Fori(0, NG // 2 - 1) as i:
                    load(i * 2 + 2, 0)
                    load(i * 2 + 3, 1)

            LOADS = 4 * 16

            @block.gpsimd
            def _(pool):
                def weights(g, jh):
                    if not (isinstance(g, int) and g < 1):
                        pool.wait_ge(sum_done, g * CK + (CK // JH * (jh + 1) - CK))
                    half = GB * T * 32
                    for q in range(Q):
                        src = wE[JW * q:JW * q + JW, bass.ds(g * GE + GB * T * jh, GB * T)].rearrange("p (g h t) -> p g h t", g=GB, h=2)
                        whole = wblk[JW * q:JW * q + JW, half * jh:half * jh + half]
                        dst = bass.AP(whole.tensor, whole.offset + 8 * q,
                                      [list(whole.ap[0]), [T * 32, GB], [8 * 32, 2], [33, 8]])
                        pool.tensor_copy(dst, src).then_inc(w_blk, 1)
                        pool.wait_ge(w_blk, g * (2 * Q) + (Q * jh + q + 1))

                def group(g, par, last=False):
                    weights(g, 0)
                    if not last:
                        copy_x(pool, g + 1)
                        split_x(pool, g + 1, 1 - par)
                    weights(g, 1)

                group(0, 0)
                with pool.Fori(0, NG // 2 - 1) as i:
                    group(i * 2 + 1, 1)
                    group(i * 2 + 2, 0)
                group(NG - 1, 1, last=True)

            @block.tensor
            def _(pe):
                def gather(g, c):
                    jh, t0 = chunk(c)
                    if c % (CK // JH) == 0:
                        pe.wait_ge(op_in[jh], g * LOADS + LOADS)
                    k = g * CK + c
                    if not (isinstance(k, int) and k < 2):
                        pe.wait_ge(z_ready, k - 1)
                    for j in range(CT):
                        t = t0 + j
                        tb = t // (T // TB)
                        ins = pe.matmul(hbuf[c % 2][:, GB * D * j:GB * D * j + GB * D], pick[jh][0:R_END, P * t:P * t + P],
                                        nodes[jh][0:R_END, GB * D * tb:GB * D * tb + GB * D], start=True, stop=True)
                    ins.then_inc(h_ready, 1)

                def weigh(g, par, c):
                    jh, t0 = chunk(c)
                    pe.wait_ge(g_ready, g * CK + (c + 1))
                    if c % (CK // JH) == 0:
                        pe.wait_ge(w_blk, g * (2 * Q) + Q * (jh + 1))
                    if c == 0 and not (isinstance(g, int) and g < 2):
                        pe.wait_ge(gs_ready, g - 1)
                    for j in range(CT):
                        t = t0 + j
                        hf = t // 8
                        for a in range(GB):
                            blk = ((jh * GB + a) * T + t) * 32
                            ins = pe.matmul(psS[par][32 * a:32 * a + 32, D * hf:D * hf + D], wblk[:, blk:blk + 32],
                                            z[c % RING][:, GB * D * j + D * a:GB * D * j + D * a + D],
                                            start=(c == 0 and j == 0), stop=(jh == 1 and t % 8 == 7), skip_group_check=True)
                    ins.then_inc(sum_done, 1)

                def turn(g):
                    pe.wait_ge(gs_ready, g + 1)
                    if not (isinstance(g, int) and g < 1):
                        pe.wait_ge(gsT_ready, g)
                    for hf in range(2):
                        ins = pe.transpose(psT[:, P * hf:P * hf + P], gs[:, D * hf:D * hf + D], ident)
                    ins.then_inc(gsT_psum, 1)

                def group(g, par, first=False, last=False):
                    for c in range(CK):
                        gather(g, c)
                        if c in OPERAND and not last:
                            for a in OPERAND[c]:
                                operand(pe, g + 1, a)
                        if c >= LAG:
                            weigh(g, par, c - LAG)
                        elif not first:
                            weigh(g - 1, 1 - par, c + CK - LAG)
                        if c == TURN and not first:
                            turn(g - 1)

                group(0, 0, first=True)
                with pe.Fori(0, NG // 2 - 1) as i:
                    group(i * 2 + 1, 1)
                    group(i * 2 + 2, 0)
                group(NG - 1, 1, last=True)
                for c in range(CK - LAG, CK):
                    weigh(NG - 1, 1, c)
                turn(NG - 1)

            @block.vector
            def _(v):
                def group(g, par, half):
                    for c in range(CK):
                        jh, t0 = chunk(c)
                        k = g * CK + c
                        v.wait_ge(h_ready, k + 1)
                        if not (isinstance(k, int) and k < RING):
                            v.wait_ge(sum_done, k - (RING - 1))
                        r = rE[:, bass.ds(g * GE + GB * T * jh, GB * T)].rearrange("p (g t) -> p t g", t=T)[:, t0:t0 + CT, :]
                        v.tensor_tensor(z[c % RING].rearrange("p (t g f) -> p t g f", g=GB, f=D),
                                        hbuf[c % 2].rearrange("p (t g f) -> p t g f", g=GB, f=D),
                                        r.unsqueeze(3).broadcast_to([P, CT, GB, D]), ALU.mult).then_inc(z_ready, 1)
                steps(v, NG, group, 2, 0)

            @block.scalar
            def _(act):
                def sums(g, par):
                    act.wait_ge(sum_done, g * CK + CK)
                    if not (isinstance(g, int) and g < 1):
                        act.wait_ge(gsT_psum, g)
                    act.copy(gs[:], psS[par][:, 0:2 * D]).then_inc(gs_ready, 1)

                def keep(g):
                    act.wait_ge(gsT_psum, g + 1)
                    for hf in range(2):
                        dst = gsT[:, bass.ds(g * (GB * N), GB * N)].rearrange("p (g h t q) -> p h g q t", g=GB, h=2, q=Q)[:, hf]
                        ins = act.copy(dst, psT[:, P * hf:P * hf + P].rearrange("p (g q t) -> p g q t", g=GB, q=Q))
                    ins.then_inc(gsT_ready, 1)

                def group(g, par, first=False, last=False):
                    for c in range(CK):
                        act.wait_ge(z_ready, g * CK + (c + 1))
                        act.activation(z[c % RING], z[c % RING], ACT.Gelu).then_inc(g_ready, 1)
                        if c == LAG - 1 and not first:
                            sums(g - 1, 1 - par)
                        if c == max(OPERAND) and not last:
                            keep_x(act, g + 1, 1 - par)
                        if c == TURN + 1 and not first:
                            keep(g - 1)

                group(0, 0, first=True)
                with act.Fori(0, NG // 2 - 1) as i:
                    group(i * 2 + 1, 1)
                    group(i * 2 + 2, 0)
                group(NG - 1, 1, last=True)
                sums(NG - 1, 1)
                keep(NG - 1)

        hc = hT
        adm = [big[:, CH * i:CH * i + CH] for i in range(4)]
        stats = wblk[:, 0:NC * PAIRS * 6]
        lnr, lnv, lnt = (wblk[:, 512 + 64 * i:576 + 64 * i] for i in range(3))
        ad_in = [sem(f"ad_in{i}") for i in range(4)]
        n_psum, n_done, ln_step, ln_var, ln_sd = map(sem, ("n_psum", "n_done", "ln_step", "ln_var", "ln_sd"))
        with nc.Block() as block:
            @block.sync
            def _(sp):
                for k in range(NC):
                    if k >= 4:
                        sp.wait_ge(n_psum, k - 3)
                    sp.dma_start(adm[k % 4], adM_d[k]).then_inc(ad_in[k % 4], 16)

            @block.tensor
            def _(pe):
                for k in range(NC):
                    pe.wait_ge(ad_in[k % 4], 16 * (k // 4 + 1))
                    if k >= 2:
                        pe.wait_ge(n_done, k - 1)
                    for c in range(PAIRS):
                        o = bank[k % 2][:, P * c:P * c + P]
                        at = slice(CH * k + P * c, CH * k + P * c + P)
                        pe.matmul(o, x1T[:, at], wt["Wna"][:], start=(c == 0), stop=False, skip_group_check=True)
                        pe.matmul(o, hT[:, at], wt["Wmsg"][:], start=False, stop=False, skip_group_check=True)
                        last = pe.matmul(o, adm[k % 4][:, P * c:P * c + P], vmsg[:], start=False, stop=True, skip_group_check=True)
                    last.then_inc(n_psum, 1)

            @block.vector
            def _(v):
                for k in range(NC):
                    v.wait_ge(n_psum, k + 1)
                    v.tensor_tensor(hc[:, CH * k:CH * k + CH].rearrange("p (c d) -> p c d", d=D),
                                    bank[k % 2][:].rearrange("p (c d) -> p c d", d=D),
                                    bn1_b[:].unsqueeze(1).broadcast_to([P, PAIRS, D]), ALU.add).then_inc(n_done, 1)
                    v.wait_ge(n_done, k + 1)
                    for c in range(PAIRS * k, PAIRS * k + PAIRS):
                        last = v.bn_stats(stats[:, 6 * c:6 * c + 6], hc[:, D * c:D * c + D])
                last.then_inc(ln_step, 1)
                v.wait_ge(ln_step, 1)
                me, ve, mo, vo = (stats.rearrange("p (b s) -> p b s", s=6)[:, :, i] for i in (1, 2, 4, 5))
                v.tensor_tensor(lnt, me, mo, ALU.subtract)
                v.tensor_tensor(lnv, ve, vo, ALU.add).then_inc(ln_step, 1)
                v.wait_ge(ln_step, 2)
                v.tensor_tensor(lnt, lnt, lnt, ALU.mult)
                v.tensor_scalar(lnv, lnv, 1.0 / D, None, ALU.mult).then_inc(ln_step, 1)
                v.wait_ge(ln_step, 3)
                v.scalar_tensor_tensor(out=lnv, in0=lnt, scalar=0.25, in1=lnv, op0=ALU.mult, op1=ALU.add).then_inc(ln_var, 1)
                v.wait_ge(ln_sd, 1)
                v.reciprocal(lnr, lnt)

            @block.scalar
            def _(act):
                act.wait_ge(ln_var, 1)
                act.activation(lnt, lnv, ACT.Sqrt, bias=cols[:, EPSC + 1:EPSC + 2]).then_inc(ln_sd, 1)

        hs, g2, oT, ob = ([big[:, CH * (2 * n + i):CH * (2 * n + i + 1)] for i in range(2)] for n in range(4))
        a_bank, o_bank, t_bank = ([bank[2 * n], bank[2 * n + 1]] for n in range(3))
        o_out = [sem(f"o_out{i}") for i in range(2)]
        hs_done, a_psum, g2_done, o_psum, oT_done, t_psum, ob_done = map(
            sem, ("hs_done", "a_psum", "g2_done", "o_psum", "oT_done", "t_psum", "ob_done"))
        out_rows = out.rearrange("b n d -> (b n) d")

        def rounds(eng, body):
            for k in range(4):
                body(k, k % 2, k // 2, lambda i: k - i >= 0)
            with eng.Fori(0, (NC - 4) // 2) as i:
                body(i * 2 + 4, 0, i + 2, lambda _: True)
                body(i * 2 + 5, 1, i + 2, lambda _: True)
            for k in range(NC, NC + 4):
                body(k, k % 2, k // 2, lambda i: k - i < NC)

        def after(eng, s, value):
            if not isinstance(value, int) or value > 0:
                eng.wait_ge(s, value)

        with nc.Block() as block:
            @block.vector
            def _(v):
                def body(k, p, h, stage):
                    if stage(0):
                        after(v, a_psum, k - 1)
                        r = lnr[:, bass.ds(k * PAIRS, PAIRS)].unsqueeze(2).broadcast_to([P, PAIRS, D])
                        v.tensor_tensor(hs[p].rearrange("p (c d) -> p c d", d=D),
                                        hc[:, bass.ds(k * CH, CH)].rearrange("p (c d) -> p c d", d=D), r, ALU.mult).then_inc(hs_done, 1)
                    if stage(2):
                        v.wait_ge(o_psum, k - 1)
                        after(v, t_psum, k - 3)
                        v.scalar_tensor_tensor(out=oT[p], in0=o_bank[p][:], scalar=cols[:, BN2:BN2 + 1],
                                               in1=x1T[:, bass.ds((k - 2) * CH, CH)], op0=ALU.add, op1=ALU.add).then_inc(oT_done, 1)
                rounds(v, body)

            @block.tensor
            def _(pe):
                def body(k, p, h, stage):
                    o = 1 - p
                    if stage(0):
                        pe.wait_ge(hs_done, k + 1)
                        after(pe, g2_done, k - 1)
                        for c in range(PAIRS):
                            last = pe.transpose(a_bank[p][:, P * c:P * c + P], hs[p][:, P * c:P * c + P], ident)
                        last.then_inc(a_psum, 1)
                    if stage(1):
                        pe.wait_ge(g2_done, k)
                        after(pe, oT_done, k - 2)
                        pe.matmul(o_bank[o][:], wt["Wn2"][:], g2[o], start=True, stop=True).then_inc(o_psum, 1)
                    if stage(3):
                        pe.wait_ge(oT_done, k - 2)
                        after(pe, ob_done, k - 4)
                        for c in range(PAIRS):
                            last = pe.transpose(t_bank[o][:, P * c:P * c + P], oT[o][:, P * c:P * c + P], ident)
                        last.then_inc(t_psum, 1)
                rounds(pe, body)

            @block.scalar
            def _(act):
                def body(k, p, h, stage):
                    o = 1 - p
                    if stage(0):
                        act.wait_ge(a_psum, k + 1)
                        after(act, o_psum, k - 1)
                        act.activation(g2[p], a_bank[p][:], ACT.Gelu, scale=cols[:, GN:GN + 1],
                                       bias=cols[:, BGN:BGN + 1]).then_inc(g2_done, 1)
                    if stage(3):
                        act.wait_ge(t_psum, k - 2)
                        after(act, o_out[o], (h - 2 if p == 0 else h - 1) * 16)
                        act.copy(ob[o], t_bank[o][:]).then_inc(ob_done, 1)
                rounds(act, body)

            @block.sync
            def _(sp):
                def body(k, p, h, stage):
                    if stage(3):
                        sp.wait_ge(ob_done, k - 2)
                        sp.dma_start(out_rows[bass.ds((k - 3) * CH, CH), :].rearrange("(c p) d -> p c d", p=P),
                                     ob[1 - p].rearrange("p (c d) -> p c d", d=D)).then_inc(o_out[1 - p], 16)
                rounds(sp, body)
                for p in range(2):
                    sp.wait_ge(o_out[p], 16 * (NC // 2))


NAMES = ["L0_gnn_W", "L0_gnn_b", "L0_gnn_gamma", "L0_gnn_beta", "L1_gnn_We1", "L1_gnn_be1", "L1_gnn_ge", "L1_gnn_bge",
         "L1_gnn_We2", "L1_gnn_be2", "L1_gnn_Wn1", "L1_gnn_bn1", "L1_gnn_gn", "L1_gnn_bgn", "L1_gnn_Wn2", "L1_gnn_bn2"]


def kernel(**inputs):
    import concourse.bacc as bacc
    from concourse.bass_utils import run_bass_kernel_spmd

    nc = bacc.Bacc("TRN2", target_bir_lowering=False, num_devices=1)
    arrays = {f"in_{n}": np.ascontiguousarray(inputs[n]) for n in ["x", "adj"] + NAMES}
    arrays["in_consts"] = constants()
    ap = {n: nc.dram_tensor(n, a.shape, mybir.dt.from_np(a.dtype), kind="ExternalInput").ap() for n, a in arrays.items()}
    out = nc.dram_tensor("out", (NB, N, D), F32, kind="ExternalOutput").ap()
    build(nc, ap["in_x"], ap["in_adj"], ap["in_consts"], {n: ap[f"in_{n}"] for n in NAMES}, out)
    r = run_bass_kernel_spmd(nc, [arrays], core_ids=[0])
    return r.results[0]["out"]
```
